# Optimizing a Trainium2 kernel written in Bass

```python
import numpy as np
import jax
import jax.numpy as jnp

def _softmax(x, axis=-1):
    return jax.nn.softmax(x, axis=axis)

def _gelu(x):
    return jax.nn.gelu(x, approximate=True)

def _silu(x):
    return jax.nn.silu(x)

def _sigmoid(x):
    return jax.nn.sigmoid(x)

def _layernorm(x, axis=-1, eps=1e-05):
    m = jnp.mean(x, axis=axis, keepdims=True)
    v = jnp.var(x, axis=axis, keepdims=True)
    return (x - m) / jnp.sqrt(v + eps)

def _scatter_add(tgt, idx, src, axis=0):
    return tgt.at[idx].add(src)

def _segment_sum(src, seg, n):
    return jax.ops.segment_sum(src, seg, n)
kernel_name = 'mk_flamingo_gated_d1_seqx_r2_a76be5'

def setup_inputs(seed: int=0):
    np.random.seed(seed)
    _w = jnp.asarray

    def _rec_inputs():
        import jax
        import jax.numpy as jnp
        _rk = jax.random.key(seed)
        x = 0.0003765 + 1 * jax.random.normal(jax.random.fold_in(_rk, 1), (16, 512, 1024), jnp.float32)
        _lenS = 512 - jax.random.randint(jax.random.fold_in(_rk, 7), (16,), 0, max(1, 512 // 4) + 1, jnp.int32)
        _lenS2 = 512 - jax.random.randint(jax.random.fold_in(_rk, 8), (16,), 0, max(1, 512 // 4) + 1, jnp.int32)
        _ctx_2048P = jax.random.normal(jax.random.fold_in(_rk, 11), (16, 16, 1024), jnp.float32)
        _ctx_2048c = jax.random.dirichlet(jax.random.fold_in(_rk, 511), 0.3 * jnp.ones((16,), jnp.float32), (16, 512))
        _ctx_2048t = jnp.einsum('bsk,bkd->bsd', _ctx_2048c, _ctx_2048P)
        _ctx_2048t = _ctx_2048t * jax.lax.rsqrt(jnp.mean(jnp.square(_ctx_2048t)) + 1e-12) * 0.953939
        ctx_2048 = -0.000292821 + 1.00034 * (_ctx_2048t + 0.3 * jax.random.normal(jax.random.fold_in(_rk, 611), (16, 512, 1024), jnp.float32))
        _g = jax.random.normal(jax.random.fold_in(_rk, 9001), (2, 1), jnp.float32)
        _g = jnp.sign(_g) * jnp.maximum(jnp.abs(_g), 1.0) + (_g == 0) * 1.0
        g_xattn = _g[0]
        g_ffn = _g[1]
        return (x, ctx_2048, g_xattn, g_ffn)
    x, ctx_2048, g_xattn, g_ffn = _rec_inputs()

    def _L0_xattn_setup():
        import jax, jax.numpy as jnp
        import numpy as np
        key = jax.random.key(seed)
        k1, k2, k3, k4, k5 = jax.random.split(key, 5)
        B, D_MODEL, L = (2, 512, 1024)
        HEAD_DIM = 8
        H = D_MODEL // HEAD_DIM
        return {'k': jax.random.normal(k1, (B, D_MODEL, L), dtype=jnp.float32), 'v': jax.random.normal(k2, (B, D_MODEL, L), dtype=jnp.float32), 'q': jax.random.normal(k3, (B, D_MODEL, L), dtype=jnp.float32), 'ssm_kernel': jax.random.normal(k4, (H, L), dtype=jnp.float32), 'D': jax.random.normal(k5, (H,), dtype=jnp.float32), 'head_dim': HEAD_DIM}
    _L0_xattn_all = _L0_xattn_setup()
    _L0_xattn_in = {k: v for k, v in _L0_xattn_all.items() if k in ('ssm_kernel', 'D')}
    del _L0_xattn_all

    def _L0_ffn_setup():
        import jax, jax.numpy as jnp
        import numpy as np
        B, S, D = (4, 2048, 1024)
        DFF = 4 * D
        CAPACITY = 0.125
        K = int(CAPACITY * S)
        key = jax.random.key(seed)
        ks = jax.random.split(key, 8)
        sc = 1.0 / np.sqrt(D)
        return {'x': jax.random.normal(ks[0], (B, S, D), dtype=jnp.float32), 'W_r': jax.random.normal(ks[1], (D, 1), dtype=jnp.float32) * sc, 'b_r': jnp.zeros((1,), dtype=jnp.float32), 'W1': jax.random.normal(ks[2], (D, DFF), dtype=jnp.float32) * sc, 'b1': jnp.zeros((DFF,), dtype=jnp.float32), 'W2': jax.random.normal(ks[3], (DFF, D), dtype=jnp.float32) * (1.0 / np.sqrt(DFF)), 'b2': jnp.zeros((D,), dtype=jnp.float32), 'position_ids': jnp.arange(B * S, dtype=jnp.int64 if jax.config.jax_enable_x64 else jnp.int32).reshape(B, S), 'cache_position': jnp.arange(S, dtype=jnp.int64 if jax.config.jax_enable_x64 else jnp.int32)}
    _L0_ffn_all = _L0_ffn_setup()
    _L0_ffn_in = {k: v for k, v in _L0_ffn_all.items() if k in ('W_r', 'b_r', 'W1', 'b1', 'W2', 'b2', 'position_ids', 'cache_position')}
    del _L0_ffn_all
    return {'x': x, 'ctx_2048': ctx_2048, 'g_xattn': g_xattn, 'g_ffn': g_ffn, 'L0_xattn_ssm_kernel': _L0_xattn_in['ssm_kernel'], 'L0_xattn_D': _L0_xattn_in['D'], 'L0_ffn_W_r': _L0_ffn_in['W_r'], 'L0_ffn_b_r': _L0_ffn_in['b_r'], 'L0_ffn_W1': _L0_ffn_in['W1'], 'L0_ffn_b1': _L0_ffn_in['b1'], 'L0_ffn_W2': _L0_ffn_in['W2'], 'L0_ffn_b2': _L0_ffn_in['b2'], 'L0_ffn_position_ids': _L0_ffn_in['position_ids'], 'L0_ffn_cache_position': _L0_ffn_in['cache_position']}

def reference(x, ctx_2048, g_xattn, g_ffn, L0_xattn_ssm_kernel, L0_xattn_D, L0_ffn_W_r, L0_ffn_b_r, L0_ffn_W1, L0_ffn_b1, L0_ffn_W2, L0_ffn_b2, L0_ffn_position_ids, L0_ffn_cache_position):
    import jax
    import jax.numpy as jnp

    def _L0_xattn_ref(k, v, q, ssm_kernel, D, head_dim):
        import jax, jax.numpy as jnp
        import numpy as np
        B, HD, L = k.shape
        H = HD // head_dim
        fft_size = 2 * L
        k_ = k.reshape(B, H, head_dim, L)
        v_ = v.reshape(B, H, head_dim, L)
        q_ = q.reshape(B, H, head_dim, L)
        kv = jnp.einsum('bhil,bhjl->bijhl', k_, v_)
        kv_f = jnp.fft.rfft(kv, n=fft_size)
        kernel_f = jnp.fft.rfft(ssm_kernel, n=fft_size)
        y = jnp.fft.irfft(kv_f * kernel_f, n=fft_size)[..., :L]
        out = y + kv * D[None, None, None, :, None]
        out = jnp.einsum('bijhl,bhil->bjhl', out, q_)
        out = jnp.transpose(out, (0, 2, 1, 3)).reshape(B, H * head_dim, L)
        return out.astype(k.dtype)

    def _L0_ffn_ref(x, W_r, b_r, W1, b1, W2, b2, position_ids, cache_position):
        import jax, jax.numpy as jnp
        import numpy as np
        B, S, D = (4, 2048, 1024)
        DFF = 4 * D
        CAPACITY = 0.125
        K = int(CAPACITY * S)
        b, s, d = x.shape
        weights = jnp.einsum('bsd,do->bso', x, W_r).squeeze(-1) + b_r
        topk_vals, topk_idx = jax.lax.top_k(weights, K)
        threshold = topk_vals[:, -1]
        sel_mask = weights > threshold[:, None]
        xg = jnp.take_along_axis(x, topk_idx[..., None], axis=1)
        h = jax.nn.gelu(jnp.einsum('bkd,df->bkf', xg, W1) + b1)
        blk = jnp.einsum('bkf,fd->bkd', h, W2) + b2
        gate = (topk_vals > threshold[:, None]).astype(x.dtype)
        wg = jnp.take_along_axis(weights, topk_idx, axis=1)
        vals = blk * (wg * gate)[..., None]
        bidx = jnp.arange(b)[:, None]
        processed = jnp.zeros_like(x).at[bidx, topk_idx].add(vals)
        return processed + x * (~sel_mask)[..., None].astype(x.dtype)
    x = x + jnp.tanh(g_xattn[0]) * _L0_xattn_ref(ctx_2048, ctx_2048, _layernorm(x, axis=-1), L0_xattn_ssm_kernel, L0_xattn_D, 8)
    x = x + jnp.tanh(g_ffn[0]) * _L0_ffn_ref(_layernorm(x, axis=-1), L0_ffn_W_r, L0_ffn_b_r, L0_ffn_W1, L0_ffn_b1, L0_ffn_W2, L0_ffn_b2, L0_ffn_position_ids, L0_ffn_cache_position)
    return x

_drawn_inputs = setup_inputs


def setup_inputs(seed=0):
    import zlib

    import numpy as np

    out = dict(_drawn_inputs(seed))
    spreads = {'L0_ffn_b1': (0.0, 0.8), 'L0_ffn_b2': (0.0, 2.0)}
    factors = {'L0_ffn_W_r': 5.354, 'L0_ffn_W1': 7.858, 'L0_ffn_W2': 7.116}
    for name, (base, spread) in spreads.items():
        noise = np.random.default_rng([zlib.crc32(name.encode()), seed]).standard_normal(out[name].shape)
        drawn = base * np.exp(spread * noise) if base else spread * noise
        out[name] = jnp.asarray(drawn.astype(out[name].dtype))
    for name, factor in factors.items():
        out[name] = (out[name] * factor).astype(out[name].dtype)
    return out
```

```python
from contextlib import ExitStack

import concourse.bass as bass
from concourse import mybir

F32, F32R, F16, I32 = mybir.dt.float32, mybir.dt.float32r, mybir.dt.float16, mybir.dt.int32
ALU = mybir.AluOpType
ACT = mybir.ActivationFunctionType
AX_X = mybir.AxisListType.X
P = 128
EXPONENT = 0x7F800000
TINY = 1e-30
EPS = 1e-5


class Chain:

    def __init__(self, engine, sem):
        self.engine, self.sem, self.base, self.off = engine, sem, 0, 0

    def start(self, base):
        self.base, self.off = base, 0

    def mark(self, instruction):
        instruction.then_inc(self.sem, 1)
        self.off += 1
        return self.off

    def sync(self):
        self.engine.wait_ge(self.sem, self.base + self.off)


def settle(engine, passed):
    engine.sem_inc(passed, 1)


def build(nc, x, ctx, g_xattn, g_ffn, kern, D, W_r, b_r, W1, b1, W2, b2, out):
    B, S, L = x.shape
    H = kern.shape[0]
    HD = S // H
    GR = P // HD
    NG = H // GR
    BH = B // 2
    NL = L // P
    PAIRS = HD * (HD + 1) // 2
    COLS = BH * PAIRS
    LB = NL * BH
    HALF = NL // 2
    STAGES = 2 * NG
    PADK = P + L
    DFF = W1.shape[1]
    KSEL = 256
    TT = S // P
    SLOTS = B * KSEL // P

    kpad = nc.dram_tensor("kpad", [2, H, PADK], F16).ap()
    kinv = nc.dram_tensor("kinv", [H, HD], F32).ap()
    x1 = nc.dram_tensor("x1", [B * S, L], F32).ap()
    xn = nc.dram_tensor("xn", [B * S, L], F32).ap()
    wall = nc.dram_tensor("wall", [B, S], F32).ap()
    xr = x.rearrange("b s l -> (b s) l")
    cr = ctx.rearrange("b s l -> (b s) l")
    outr = out.rearrange("b s l -> (b s) l")

    top = ExitStack()
    with top:
        ident = top.enter_context(nc.sbuf_tensor("ident", [P, P], F32))
        gates = top.enter_context(nc.sbuf_tensor("gates", [P, 4], F32))
        kinv_col = top.enter_context(nc.sbuf_tensor("kinv_col", [P, NG], F32))
        slot_row = top.enter_context(nc.sbuf_tensor("slot_row", [P, SLOTS], I32))
        slot_gate = top.enter_context(nc.sbuf_tensor("slot_gate", [P, SLOTS], F32))
        tg_x, tg_f = gates[:, 2:3], gates[:, 3:4]
        setup(nc, H, L, HD, PADK, NG, kern, D, g_xattn, g_ffn, kpad, kinv, ident, gates, kinv_col)
        conv(nc, locals())
        route(nc, locals())
        experts(nc, locals())


def setup(nc, H, L, HD, PADK, NG, kern, D, g_xattn, g_ffn, kpad, kinv, ident, gates, kinv_col):
    with ExitStack() as c:
        def sb(n, s, d): return c.enter_context(nc.sbuf_tensor(n, s, d))
        def sem(n): return c.enter_context(nc.semaphore(n))
        K = sb("K", [H, L], F32)
        Ks = sb("Ks", [H, L], F32)
        Dc = sb("Dc", [H, 1], F32)
        Kh = sb("Kh", [H, PADK], F16)
        Kl = sb("Kl", [H, PADK], F16)
        m = sb("km", [H, 4], F32)
        inv8 = sb("inv8", [H, HD], F32)
        inputs_in, gates_in = sem("inputs_in"), sem("gates_in")
        step, ident_ready = sem("setup_step"), sem("ident_ready")
        parts_ready, parts_out, inv_in = sem("parts_ready"), sem("parts_out"), sem("inv_in")
        tanh_done = sem("tanh_done")
        block = c.enter_context(nc.Block())

        @block.sync
        def _(sp):
            sp.dma_start(K[:], kern).then_inc(inputs_in, 16)
            sp.dma_start(Dc[:], D.rearrange("(h a) -> h a", a=1)).then_inc(inputs_in, 16)
            sp.dma_start(gates[:, 0:1], bass.AP(g_xattn.tensor, 0, [[0, P], [1, 1]])).then_inc(gates_in, 16)
            sp.dma_start(gates[:, 1:2], bass.AP(g_ffn.tensor, 0, [[0, P], [1, 1]])).then_inc(gates_in, 16)
            sp.wait_ge(parts_ready, 1)
            sp.dma_start(kpad[0], Kh[:]).then_inc(parts_out, 16)
            sp.dma_start(kpad[1], Kl[:]).then_inc(parts_out, 16)
            sp.dma_start(kinv, inv8[:]).then_inc(parts_out, 16)
            sp.wait_ge(parts_out, 48)
            with nc.allow_non_contiguous_dma("a few words"):
                sp.dma_start(kinv_col[:], bass.AP(kinv.tensor, 0, [[1, P], [P, NG]])).then_inc(inv_in, 16)
            sp.wait_ge(inv_in, 16)

        @block.scalar
        def _(act):
            act.wait_ge(gates_in, 32)
            nc.scalar.activation(gates[:, 2:4], gates[:, 0:2], ACT.Tanh).then_inc(tanh_done, 1)

        @block.gpsimd
        def _(pool):
            nc.gpsimd.memset(ident[:], 0.0).then_inc(ident_ready, 1)
            pool.wait_ge(ident_ready, 1)
            nc.gpsimd.affine_select(out=ident[:], in_=ident[:], compare_op=ALU.not_equal, fill=1.0, base=0,
                                    pattern=[[-1, P]], channel_multiplier=1).then_inc(ident_ready, 1)

        @block.vector
        def _(dve):
            ch = Chain(dve, step)
            V = nc.vector
            ch.mark(V.memset(Kh[:, 0:P], 0.0))
            ch.mark(V.memset(Kl[:, 0:P], 0.0))
            dve.wait_ge(inputs_in, 32)
            ch.mark(V.tensor_tensor(K[:, 0:1], K[:, 0:1], Dc[:], ALU.add)); ch.sync()
            ch.mark(V.tensor_reduce(m[:, 0:1], K[:], AX_X, ALU.max, apply_absolute_value=True)); ch.sync()
            ch.mark(V.tensor_scalar(m[:, 1:2], m[:, 0:1], TINY, None, ALU.max)); ch.sync()
            ch.mark(V.tensor_scalar(m[:, 2:3].bitcast(I32), m[:, 1:2].bitcast(I32), EXPONENT, None,
                                    ALU.bitwise_and)); ch.sync()
            ch.mark(V.reciprocal(m[:, 3:4], m[:, 2:3])); ch.sync()
            ch.mark(V.tensor_scalar(Ks[:], K[:], m[:, 3:4], 8192.0, ALU.mult, ALU.mult)); ch.sync()
            ch.mark(V.tensor_copy(Kh[:, P:PADK], Ks[:])); ch.sync()
            ch.mark(V.tensor_tensor(Kl[:, P:PADK], Ks[:], Kh[:, P:PADK], ALU.subtract))
            ch.mark(V.memset(inv8[:], 1.0 / 8192.0)); ch.sync()
            V.tensor_scalar(inv8[:], inv8[:], m[:, 2:3], None, ALU.mult).then_inc(parts_ready, 1)


def conv(nc, v):
    B, S, L, H, HD, GR, NG, BH, NL = (v[k] for k in ("B", "S", "L", "H", "HD", "GR", "NG", "BH", "NL"))
    PAIRS, COLS, HALF, STAGES, PADK = (v[k] for k in ("PAIRS", "COLS", "HALF", "STAGES", "PADK"))
    kpad, x1, xr, cr = (v[k] for k in ("kpad", "x1", "xr", "cr"))
    ident, kinv_col, tg_x = v["ident"], v["kinv_col"], v["tg_x"]
    HLB = HALF * BH
    FULL = HD // 2
    WRAP = HD + FULL - 1
    assert PAIRS == FULL * HD + FULL
    LB = NL * BH
    YB = 4
    UP = GR // 2
    assert UP == BH
    C_TURNED, C_MOVED, C_DONE, C_YMOVED, C_YUSED, C_LOW, C_BACK, C_KV = 4, 2, 2 * NL, YB, 2, 2, 2, 2
    with ExitStack() as c:
        def sb(n, s, d): return c.enter_context(nc.sbuf_tensor(n, s, d))
        def pb(n, s): return c.enter_context(nc.psum_tensor(n, s, F32))
        def sem(n): return c.enter_context(nc.semaphore(n))
        ctxT_all = sb("ctxT", [P, 2, NL, BH, P], F32)
        ctxT = [ctxT_all[:, k] for k in range(2)]
        qT = [sb(f"qT{k}", [P, NL, BH, P], F32) for k in range(2)]
        kv = [sb(f"kv{k}", [P, HALF, BH, PAIRS], F32) for k in range(2)]
        kvh = [sb(f"kvh{k}", [P, NL, BH, PAIRS], F16) for k in range(2)]
        kvl = [sb(f"kvl{k}", [P, NL, BH, PAIRS], F16) for k in range(2)]
        y = [sb(f"y{k}", [P, HALF, BH, PAIRS], F32) for k in range(2)]
        cx = [sb(f"cx{k}", [P, HLB, WRAP], F32) for k in range(2)]
        qx = [sb(f"qx{k}", [P, HLB, WRAP], F32) for k in range(2)]
        prod = sb("prod", [P, HLB, HD * HD], F32)
        toep = [sb(f"toep{k}", [P, 2, L], F16) for k in range(2)]
        c_row = sb("c_row", [P, L], F32)
        x_row = sb("x_row", [P, L], F32)
        s_row = sb("s_row", [P, L], F32)
        f_row = sb("f_row", [P, L], F32)
        staged = sb("staged", [P, NL, P], F32)
        coef = sb("coef", [P, 2, BH], F32)
        st = sb("st", [P, 2, 6], F32)
        sc = sb("sc", [P, 12], F32)
        y_ps = [pb(f"y_ps{k}", [P, 512]) for k in range(YB)]
        t_ps = [pb(f"t_ps{k}", [P, 4, P]) for k in range(2)]
        f_ps = [pb(f"f_ps{k}", [P, 4, P]) for k in range(2)]

        ctx_in, x_in, fx_in, x1_out = sem("ctx_in"), sem("x_in"), sem("fx_in"), sem("x1_out")
        passed = sem("passed")
        toep_in = [sem(f"toep_in{k}") for k in range(2)]
        half_step, prep_step = sem("half_step"), sem("prep_step")
        var_ready, std_ready = sem("var_ready"), sem("std_ready")
        cs_ready, q_ready = sem("cs_ready"), sem("q_ready")
        cx_ready = sem("cx_ready")
        turned, turned_moved = sem("turned"), sem("turned_moved")
        kv_ready, kvh_ready, kvl_ready = sem("kv_ready"), sem("kvh_ready"), sem("kvl_ready")
        y_done, y_moved, y_used = sem("y_done"), sem("y_moved"), sem("y_used")
        out_ready, staged_ready, back, x1_ready = sem("out_ready"), sem("staged_ready"), sem("back"), sem("x1_ready")
        block = c.enter_context(nc.Block())

        def stages(engine, step, prepare, finish, begin=None):
            if prepare:
                with engine.Fori(0, UP) as u:
                    prepare(0, 0, u)
            if begin:
                begin()
            with engine.Fori(0, UP) as u:
                step(0, 0, u, False, True, True)
            with engine.Fori(0, (STAGES - 2) // 2) as sp:
                for k in range(2):
                    with engine.Fori(0, UP) as u:
                        step(2 * sp + (1 + k), (k + 1) % 2, u, True, True, True)
            with engine.Fori(0, UP - 1) as u:
                step(STAGES - 1, (STAGES - 1) % 2, u, True, False, True)
            step(STAGES - 1, (STAGES - 1) % 2, UP - 1, True, False, False)
            if finish:
                with engine.Fori(0, UP) as u:
                    finish(STAGES, STAGES % 2, u)

        def slide(t, shape):
            whole = t[:]
            step = whole.ap[0][0]
            return bass.AP(whole.tensor, whole.offset, [[step, P], [WRAP, HLB], [1, shape[2]], [1, shape[3]]])

        def rows(t, s, u):
            first = ((s // NG) * BH + u) * S + (s % NG) * P
            return t[bass.ds(first, P), :]

        @block.sync
        def _(sp):
            def load(m):
                sp.wait_ge(cs_ready, m + 1)
                sp.dma_start(c_row[:], rows(cr, (m // UP) % STAGES, m % UP)).then_inc(ctx_in, 16)
                sp.wait_ge(q_ready, m + 1)
                sp.dma_start(x_row[:], rows(xr, (m // UP) % STAGES, m % UP)).then_inc(x_in, 16)

            def kernels(n, k):
                h = ((n // GR) % NG) * GR + n % GR
                for part in range(2):
                    src = bass.AP(kpad.tensor, (h + part * H) * PADK + 1, [[1, P], [1, L]])
                    sp.dma_start(toep[k][:, part, :], src).then_inc(toep_in[k], 16)

            def fetch(s, par, u):
                n = (s - 1) * UP + u
                sp.wait_ge(x1_out, 16 * n + 16)
                sp.dma_start(f_row[:], rows(xr, s - 1, u)).then_inc(fx_in, 16)

            def store(s, par, u):
                n = (s - 1) * UP + u
                sp.wait_ge(x1_ready, 1 + n + 1)
                sp.dma_start(rows(x1, s - 1, u), f_row[:]).then_inc(x1_out, 16)

            def step(s, par, u, fin, prep, more):
                if fin:
                    fetch(s, par, u)
                for k in range(2):
                    n = s * GR + 2 * u + k
                    if more:
                        sp.wait_ge(y_done, C_DONE + NL * n + NL)
                        kernels(n + 2, k)
                    if k == 0 and prep:
                        load((s + 1) * UP + u + 1)
                if fin:
                    store(s, par, u)

            def last(s, par, u):
                fetch(s, par, u)
                store(s, par, u)

            def begin():
                load(UP)
                kernels(0, 0)
                kernels(1, 1)

            sp.sem_inc(x1_out, 16)
            stages(sp, step, lambda s, par, u: load(u), last, begin)
            sp.wait_ge(x1_out, 16 * STAGES * UP + 16)

        @block.gpsimd
        def _(pool):
            G = nc.gpsimd

            def step(s, par, u, fin, prep, more):
                for k in range(2):
                    n = s * GR + 2 * u + k

                    def products(half):
                        pool.wait_ge(cx_ready, 2 * n + half + 1)
                        pool.wait_ge(kvl_ready, C_LOW + 2 * n + half - 1)
                        dst = kv[half][:].rearrange("p a b r -> p (a b) r")
                        both = [P, HLB, FULL, HD]
                        G.tensor_tensor(dst[:, :, 0:FULL * HD].rearrange("p a (d i) -> p a d i", d=FULL),
                                        cx[half][:, :, 0:HD].rearrange("p a (d i) -> p a d i", d=1).broadcast_to(both),
                                        slide(cx[half], both), ALU.mult)
                        G.tensor_tensor(dst[:, :, FULL * HD:PAIRS], cx[half][:, :, 0:FULL], cx[half][:, :, FULL:HD],
                                        ALU.mult).then_inc(kv_ready, 1)

                    def low(half):
                        pool.wait_ge(kvh_ready, 2 * n + half + 1)
                        a = slice(half * HALF, (half + 1) * HALF)
                        G.tensor_tensor(kvl[k][:, a], kv[half][:], kvh[k][:, a], ALU.subtract).then_inc(kvl_ready, 1)

                    products(0)
                    products(1)
                    pool.wait_ge(y_done, C_DONE + NL * n - NL)
                    low(0)
                    low(1)

            pool.sem_inc(kvl_ready, C_LOW)
            pool.sem_inc(kv_ready, C_KV)
            stages(pool, step, None, None)

        @block.scalar
        def _(act):
            A = nc.scalar

            def root(s, par, u):
                n = s * UP + u
                act.wait_ge(var_ready, n + 1)
                A.activation(sc[:, 6:7], sc[:, 5:6], ACT.Sqrt).then_inc(std_ready, 1)

            def turn(s, par, u, groups):
                n = s * UP + u
                for g in groups:
                    dst = (ctxT if g < 2 else qT)[par]
                    a = (g % 2) * 4
                    act.wait_ge(turned, C_TURNED + 4 * n + g + 1)
                    settle(act, passed)
                    A.activation(dst[:, a:a + 4, bass.ds(u, 1), :].rearrange("p a b r -> p a (b r)"), t_ps[g % 2][:],
                                 ACT.Copy).then_inc(turned_moved, 1)

            def prepare(s, par, u):
                root(s, par, u)
                turn(s, par, u, range(4))

            def stage_out(s, par, u):
                n = (s - 1) * UP + u
                act.wait_ge(out_ready, 2 * GR * s)
                act.wait_ge(back, C_BACK + 2 * n)
                A.activation(staged[:], qT[1 - par][:, :, bass.ds(u, 1), :].rearrange("p a b r -> p a (b r)"),
                             ACT.Copy).then_inc(staged_ready, 1)

            def lay(dst, src, half, col):
                part = src[:, half * HALF:(half + 1) * HALF].rearrange("p a b r -> p (a b) r")
                A.activation(dst[half][:, :, 0:HD], part[:, :, bass.ds(col, HD)], ACT.Copy)
                return A.activation(dst[half][:, :, HD:WRAP], part[:, :, bass.ds(col, WRAP - HD)], ACT.Copy)

            def lay_ctx(n):
                first = ((n // GR) % 2) * (LB * P) + (n % GR) * HD
                for half in range(2):
                    act.wait_ge(kv_ready, C_KV + 2 * n + half - 1)
                    src = [bass.AP(ctxT_all[:].tensor, first + half * HLB * P, [[2 * LB * P, P], [P, HLB], [1, w]])
                           for w in (HD, WRAP - HD)]
                    A.activation(cx[half][:, :, 0:HD], src[0], ACT.Copy)
                    A.activation(cx[half][:, :, HD:WRAP], src[1], ACT.Copy).then_inc(cx_ready, 1)

            def high(n, k, half):
                if half == 0:
                    act.wait_ge(y_done, C_DONE + NL * n - NL)
                act.wait_ge(kv_ready, C_KV + 2 * n + half + 1)
                A.activation(kvh[k][:, half * HALF:(half + 1) * HALF], kv[half][:],
                             ACT.Copy).then_inc(kvh_ready, 1)

            def begin():
                act.wait_ge(turned_moved, C_MOVED + 4 * UP)
                lay_ctx(0)
                lay_ctx(1)
                high(0, 0, 0)
                high(0, 0, 1)

            def step(s, par, u, fin, prep, more):
                act.wait_ge(turned_moved, C_MOVED + 4 * UP * (s + 1))
                for k in range(2):
                    n = s * GR + 2 * u + k
                    for lt in range(NL):
                        half, a = lt // HALF, lt % HALF
                        if a == 0:
                            act.wait_ge(y_used, C_YUSED + 2 * n + half - 1)
                            lay(qx, qT[par], half, (2 * u + k) * HD)
                        act.wait_ge(y_done, C_DONE + NL * n + lt + 1)
                        A.activation(y[half][:, a].rearrange("p b r -> p (b r)"), y_ps[lt % YB][:, 0:COLS],
                                     ACT.Copy).then_inc(y_moved, 1)
                        if lt == 3 and k == 0 and prep:
                            turn(s + 1, 1 - par, u, range(2))
                        if lt in (3, 5) and (more or k == 0):
                            high(n + 1, 1 - k, lt // 4)
                        if lt == 6 and more:
                            if prep:
                                act.wait_ge(turned_moved, C_MOVED + 4 * UP * (s + 1) + 4 * u + 2)
                            lay_ctx(n + 2)
                    if k == 0 and prep:
                        root(s + 1, 1 - par, u)
                    if k == 0 and fin:
                        stage_out(s, par, u)
                    if k == 1 and prep:
                        turn(s + 1, 1 - par, u, range(2, 4))

            act.sem_inc(turned_moved, C_MOVED)
            act.sem_inc(y_moved, C_YMOVED)
            stages(act, step, prepare, stage_out, begin)

        @block.vector
        def _(dve):
            V = nc.vector

            def diagonal(first, rows, width):
                whole = prod[:]
                return bass.AP(whole.tensor, whole.offset + first,
                               [[whole.ap[0][0], P], [HD * HD, HLB], [HD + 1, rows], [1, width]])

            def rows_in(s, par, u):
                n = s * UP + u
                ch = Chain(dve, prep_step)
                ch.start(14 * n + 14)
                dve.wait_ge(ctx_in, 16 * n + 16)
                ch.mark(V.tensor_reduce(sc[:, 0:1], c_row[:], AX_X, ALU.max, apply_absolute_value=True)); ch.sync()
                ch.mark(V.tensor_scalar(sc[:, 1:2], sc[:, 0:1], TINY, None, ALU.max)); ch.sync()
                ch.mark(V.tensor_scalar(sc[:, 2:3].bitcast(I32), sc[:, 1:2].bitcast(I32), EXPONENT, None,
                                        ALU.bitwise_and)); ch.sync()
                ch.mark(V.reciprocal(sc[:, 3:4], sc[:, 2:3])); ch.sync()
                dve.wait_ge(turned, C_TURNED + 4 * n)
                ch.mark(V.tensor_scalar(s_row[:, ::-1], c_row[:], sc[:, 3:4], 64.0, ALU.mult, ALU.mult))
                ch.sync()
                dve.sem_inc(cs_ready, 1)
                dve.wait_ge(x_in, 16 * n + 16)
                V.bn_stats(st[:, 0, :], x_row[:, 0:512])
                ch.mark(V.bn_stats(st[:, 1, :], x_row[:, 512:1024])); ch.sync(); settle(dve, passed)
                ch.mark(V.bn_aggr(sc[:, 4:6], st[:].rearrange("p a b -> p (a b)"))); ch.sync()
                ch.mark(V.tensor_scalar(sc[:, 5:6], sc[:, 5:6], EPS, None, ALU.add)); ch.sync()
                dve.sem_inc(var_ready, 1)
                assert ch.off == 8

            def rows_scaled(s, par, u):
                n = s * UP + u
                ch = Chain(dve, prep_step)
                ch.start(14 * n + 22)
                dve.wait_ge(std_ready, n + 1)
                ch.mark(V.reciprocal(sc[:, 7:8], sc[:, 6:7])); ch.sync()
                ch.mark(V.tensor_scalar(sc[:, 8:9], sc[:, 7:8], sc[:, 7:8], sc[:, 5:6], ALU.mult, ALU.mult)); ch.sync()
                ch.mark(V.tensor_scalar(sc[:, 9:10], sc[:, 8:9], -0.5, 1.5, ALU.mult, ALU.add)); ch.sync()
                ch.mark(V.tensor_scalar(sc[:, 10:11], sc[:, 9:10], sc[:, 7:8], sc[:, 2:3], ALU.mult, ALU.mult)); ch.sync()
                ch.mark(V.tensor_scalar(sc[:, 11:12], sc[:, 10:11], 1.0 / 64, None, ALU.mult)); ch.sync()
                dve.wait_ge(turned, C_TURNED + 4 * n + 2)
                V.tensor_scalar(s_row[:], x_row[:], sc[:, 4:5], sc[:, 11:12], ALU.subtract, ALU.mult).then_inc(q_ready, 1)
                assert ch.off == 5

            def factor(s, par, u):
                n = s * UP + u
                ch = Chain(dve, prep_step)
                ch.start(14 * n + 27)
                ch.mark(V.tensor_scalar(coef[:, par, bass.ds(u, 1)], kinv_col[:, bass.ds(s % NG, 1)], sc[:, 2:3], None,
                                        ALU.mult)); ch.sync()

            def prepare(s, par, u):
                rows_in(s, par, u)
                rows_scaled(s, par, u)
                factor(s, par, u)

            def finish(s, par, u):
                n = (s - 1) * UP + u
                dve.wait_ge(fx_in, 16 * n + 16)
                dve.wait_ge(back, C_BACK + 2 * n + 2)
                for g in range(2):
                    a = slice(512 * g, 512 * (g + 1))
                    ins = V.scalar_tensor_tensor(f_row[:, a], f_ps[g][:].rearrange("p a b -> p (a b)"),
                                                 coef[:, 1 - par, bass.ds(u, 1)], f_row[:, a], ALU.mult, ALU.add)
                ins.then_inc(x1_ready, 1)
                dve.wait_ge(x1_ready, 1 + n + 1)

            def step(s, par, u, fin, prep, more):
                dve.wait_ge(turned_moved, C_MOVED + 4 * UP * (s + 1))
                if prep:
                    rows_in(s + 1, 1 - par, u)
                for k in range(2):
                    n = s * GR + 2 * u + k
                    col = (2 * u + k) * HD
                    for half in range(2):
                        ch = Chain(dve, half_step)
                        ch.start(3 * (2 * n + half))
                        ys, q = y[half][:].rearrange("p a b r -> p (a b) r"), qx[half]
                        both = [P, HLB, FULL, HD]
                        yd = ys[:, :, 0:FULL * HD].rearrange("p a (d i) -> p a d i", d=FULL)
                        dve.wait_ge(y_moved, C_YMOVED + NL * n + HALF * (half + 1))
                        V.tensor_tensor(prod[:, :, 0:FULL * HD].rearrange("p a (d i) -> p a d i", d=FULL), yd,
                                        slide(q, both), ALU.mult)
                        V.tensor_tensor(diagonal(FULL * HD + 1, FULL - 1, HD), yd[:, :, 1:FULL],
                                        q[:, :, 0:HD].rearrange("p a (d i) -> p a d i", d=1)
                                        .broadcast_to([P, HLB, FULL - 1, HD]), ALU.mult)
                        V.tensor_tensor(prod[:, :, HD * HD - FULL:HD * HD], ys[:, :, FULL * HD:PAIRS],
                                        q[:, :, 0:FULL], ALU.mult)
                        ins = V.tensor_tensor(diagonal(FULL * HD, FULL, 1), ys[:, :, FULL * HD:PAIRS]
                                              .rearrange("p a (d i) -> p a d i", i=1),
                                              q[:, :, FULL:HD].rearrange("p a (d i) -> p a d i", i=1), ALU.mult)
                        ch.mark(ins); ch.sync()
                        dve.sem_inc(y_used, 1)
                        ch.mark(V.tensor_tensor(prod[:, :, 0:32], prod[:, :, 0:32], prod[:, :, 32:64], ALU.add)); ch.sync()
                        ch.mark(V.tensor_tensor(prod[:, :, 0:16], prod[:, :, 0:16], prod[:, :, 16:32], ALU.add)); ch.sync()
                        o = qT[par][:, half * HALF:(half + 1) * HALF].rearrange("p a b r -> p (a b) r")
                        V.tensor_tensor(o[:, :, bass.ds(col, HD)], prod[:, :, 0:HD], prod[:, :, HD:2 * HD],
                                        ALU.add).then_inc(out_ready, 1)
                        dve.wait_ge(out_ready, 2 * n + half + 1)
                    if k == 0 and prep:
                        rows_scaled(s + 1, 1 - par, u)
                if fin:
                    finish(s, par, u)
                if prep:
                    factor(s + 1, 1 - par, u)

            dve.sem_inc(cs_ready, 1)
            dve.sem_inc(q_ready, 1)
            dve.sem_inc(x1_ready, 1)
            dve.sem_inc(y_used, C_YUSED)
            V.tensor_scalar(kinv_col[:], kinv_col[:], tg_x, 1.0 / 64, ALU.mult, ALU.mult).then_inc(prep_step, 14)
            stages(dve, step, prepare, finish)

        @block.tensor
        def _(pe):
            T = nc.tensor

            def turn(s, par, u, groups):
                n = s * UP + u
                for g in groups:
                    if g % 2 == 0:
                        pe.wait_ge((cs_ready, q_ready)[g // 2], n + 2)
                    pe.wait_ge(turned_moved, C_MOVED + 4 * n + g - 1)
                    for a in range(4):
                        lt = (g % 2) * 4 + a
                        src = s_row[:, (NL - 1 - lt) * P:(NL - lt) * P] if g < 2 else s_row[:, lt * P:(lt + 1) * P]
                        ins = T.transpose(t_ps[g % 2][:, a, :], src, ident[:])
                    ins.then_inc(turned, 1)

            def prepare(s, par, u):
                turn(s, par, u, range(4))

            def finish(s, par, u):
                n = (s - 1) * UP + u
                pe.wait_ge(staged_ready, n + 1)
                pe.wait_ge(x1_ready, n + 1)
                for g in range(2):
                    for a in range(4):
                        ins = T.transpose(f_ps[g][:, a, :], staged[:, 4 * g + a, :], ident[:])
                    ins.then_inc(back, 1)

            def step(s, par, u, fin, prep, more):
                for k in range(2):
                    n = s * GR + 2 * u + k
                    pe.wait_ge(toep_in[k], 32 * (s * UP + u + 1))
                    pe.wait_ge(kvh_ready, 2 * n + 2)
                    pe.wait_ge(kvl_ready, C_LOW + 2 * n + 2)
                    for lt in range(NL):
                        pe.wait_ge(y_moved, C_YMOVED + NL * n + lt + 1 - YB)
                        for mt in range(lt + 1):
                            d = slice((lt - mt) * P, (lt - mt + 1) * P)
                            for q, (tp, kvp) in enumerate(((0, kvh), (0, kvl), (1, kvh))):
                                ins = T.matmul(y_ps[lt % YB][:, 0:COLS], toep[k][:, tp, d],
                                               kvp[k][:, mt].rearrange("p b r -> p (b r)"),
                                               start=(mt == 0 and q == 0), stop=(mt == lt and q == 2))
                        ins.then_inc(y_done, 1)
                        if lt == 3 and k == 0 and prep:
                            turn(s + 1, 1 - par, u, range(2))
                        if lt == 3 and k == 1 and fin:
                            finish(s, par, u)
                if prep:
                    turn(s + 1, 1 - par, u, range(2, 4))

            pe.sem_inc(turned, C_TURNED)
            pe.sem_inc(y_done, C_DONE)
            pe.sem_inc(back, C_BACK)
            stages(pe, step, prepare, finish)


def route(nc, v):
    B, S, L, TT, KSEL = (v[k] for k in ("B", "S", "L", "TT", "KSEL"))
    x1, xn, wall, outr, tg_f = (v[k] for k in ("x1", "xn", "wall", "outr", "tg_f"))
    W_r, b_r, slot_row, slot_gate = (v[k] for k in ("W_r", "b_r", "slot_row", "slot_gate"))
    KT = KSEL // P
    with ExitStack() as c:
        def sb(n, s, d=F32): return c.enter_context(nc.sbuf_tensor(n, s, d))
        def sem(n): return c.enter_context(nc.semaphore(n))
        x1t = [sb(f"x1t{k}", [P, TT, L]) for k in range(2)]
        xnt = [sb(f"xnt{k}", [P, TT, L]) for k in range(2)]
        w_row = [sb(f"w_row{k}", [P, S]) for k in range(2)]
        w_col = [sb(f"w_col{k}", [P, TT]) for k in range(2)]
        wr_all = sb("wr_all", [P, L])
        br_all = sb("br_all", [P, 1])
        later = sb("later", [P, TT, S])
        slots_iota = sb("slots_iota", [P, KSEL])
        hot = sb("hot", [P, TT, KSEL])
        token = sb("token", [P, TT, 2])
        junk = sb("junk", [P, L])
        st = sb("rst", [P, TT, 2, 6])
        mv = [sb(f"mv{k}", [P, TT, 2]) for k in range(2)]
        var, std, rstd, tmp = (sb(n, [P, TT]) for n in ("rvar", "rstd_inv", "rstd", "rtmp"))
        ge, eq, rank, sel, base_f = (sb(n, [P, TT]) for n in ("ge", "eq", "rank", "sel", "base_f"))
        s_ps = c.enter_context(nc.psum_tensor("s_ps", [P, KT, 2], F32))

        wr_in, x1_in, xn_out, base_out = sem("wr_in"), [sem(f"x1_in{k}") for k in range(2)], sem("xn_out"), sem("base_out")
        passed = sem("rpassed")
        w_out, w_in = sem("w_out"), sem("w_in")
        const_step, a_step, b_step = sem("const_step"), sem("a_step"), sem("b_step")
        const_ready = sem("const_ready")
        var_ready, std_ready, xn_ready, w_ready = sem("rvar_ready"), sem("rstd_ready"), sem("xn_ready"), sem("w_ready")
        hot_ready, slots_done, slots_read = sem("hot_ready"), sem("slots_done"), sem("slots_read")
        base_ready = sem("base_ready")
        block = c.enter_context(nc.Block())
        NA, NB = 11, 12

        def batches(engine, first, second):
            first(0, 0)
            with engine.Fori(0, B // 2 - 1) as j:
                for k in range(2):
                    first(2 * j + k + 1, 1 - k)
                    second(2 * j + k, k)
            first(B - 1, 1)
            second(B - 2, 0)
            second(B - 1, 1)

        def tiles(t, b):
            return t[bass.ds(b * S, S), :].rearrange("(t p) l -> p t l", p=P)

        @block.sync
        def _(sp):
            def load(b, k):
                sp.wait_ge(base_out, 16 * b + 16)
                sp.dma_start(x1t[k][:], tiles(x1, b)).then_inc(x1_in[k], 16)

            def store(b, k):
                sp.wait_ge(xn_ready, b + 1)
                sp.dma_start(tiles(xn, b), xnt[k][:]).then_inc(xn_out, 16)
                sp.wait_ge(base_ready, b + 1)
                sp.dma_start(tiles(outr, b), x1t[k][:]).then_inc(base_out, 16)

            sp.dma_start(wr_all[:], bass.AP(W_r.tensor, 0, [[0, P], [1, L]])).then_inc(wr_in, 16)
            sp.dma_start(br_all[:], bass.AP(b_r.tensor, 0, [[0, P], [1, 1]])).then_inc(wr_in, 16)
            sp.sem_inc(base_out, 32)
            batches(sp, load, store)
            sp.wait_ge(xn_out, 16 * B)
            sp.wait_ge(base_out, 16 * B + 32)

        @block.scalar
        def _(act):
            def turn(b, k):
                act.wait_ge(var_ready, b + 1)
                nc.scalar.activation(std[:], var[:], ACT.Sqrt).then_inc(std_ready, 1)
                act.wait_ge(w_ready, b + 1)
                with nc.allow_non_contiguous_dma("512 words"):
                    act.dma_start(wall[bass.ds(b, 1), :].rearrange("a (t p) -> p (a t)", p=P), w_col[k][:]).then_inc(w_out, 16)
                act.wait_ge(w_out, 16 * b + 16)
                act.dma_start(w_row[k][:], bass.AP(wall.tensor, b * S, [[0, P], [1, S]])).then_inc(w_in, 16)

            batches(act, turn, lambda b, k: None)

        @block.gpsimd
        def _(pool):
            G = nc.gpsimd
            G.memset(later[:], 1.0).then_inc(const_step, 1)
            G.iota(junk[:, 0:KSEL].bitcast(I32), pattern=[[1, KSEL]], base=0, channel_multiplier=0).then_inc(const_step, 1)
            G.iota(junk[:, KSEL:KSEL + TT].bitcast(I32), pattern=[[P, TT]], base=-S, channel_multiplier=1).then_inc(const_step, 1)
            pool.wait_ge(const_step, 3)
            G.affine_select(out=later[:], in_=later[:], compare_op=ALU.is_ge, fill=0.0, base=0,
                            pattern=[[-P, TT], [1, S]], channel_multiplier=-1).then_inc(const_ready, 1)
            G.tensor_copy(slots_iota[:], junk[:, 0:KSEL].bitcast(I32)).then_inc(const_ready, 1)
            G.tensor_copy(token[:, :, 0], junk[:, KSEL:KSEL + TT].bitcast(I32)).then_inc(const_ready, 1)

        @block.vector
        def _(dve):
            V = nc.vector

            def weigh(b, k):
                ch = Chain(dve, a_step)
                ch.start(NA * b)
                dve.wait_ge(x1_in[k], 16 * (b // 2) + 16)
                for t in range(TT):
                    V.bn_stats(st[:, t, 0, :], x1t[k][:, t, 0:512])
                    ins = V.bn_stats(st[:, t, 1, :], x1t[k][:, t, 512:1024])
                ch.mark(ins); ch.sync(); settle(dve, passed)
                for t in range(TT):
                    ins = V.bn_aggr(mv[k][:, t, :], st[:, t].rearrange("p a b -> p (a b)"))
                ch.mark(ins); ch.sync()
                V.tensor_scalar(var[:], mv[k][:, :, 1], EPS, None, ALU.add).then_inc(var_ready, 1)
                dve.wait_ge(std_ready, b + 1)
                ch.mark(V.reciprocal(rstd[:], std[:])); ch.sync()
                ch.mark(V.tensor_tensor(tmp[:], rstd[:], rstd[:], ALU.mult)); ch.sync()
                ch.mark(V.tensor_tensor(tmp[:], tmp[:], var[:], ALU.mult)); ch.sync()
                ch.mark(V.tensor_scalar(tmp[:], tmp[:], -0.5, 1.5, ALU.mult, ALU.add)); ch.sync()
                ch.mark(V.tensor_tensor(rstd[:], rstd[:], tmp[:], ALU.mult)); ch.sync()
                dve.wait_ge(xn_out, 16 * b + 16)
                for t in range(TT):
                    ins = V.tensor_scalar(xnt[k][:, t], x1t[k][:, t], mv[k][:, t, 0:1], rstd[:, t:t + 1],
                                          ALU.subtract, ALU.mult)
                ins.then_inc(xn_ready, 1)
                dve.wait_ge(xn_ready, b + 1)
                for t in range(TT):
                    ch.mark(V.tensor_tensor_reduce(out=junk[:], in0=xnt[k][:, t], in1=wr_all[:], scale=1.0, scalar=0.0,
                                                   op0=ALU.mult, op1=ALU.add, accum_out=w_col[k][:, t:t + 1]))
                    ch.sync()
                V.tensor_scalar(w_col[k][:], w_col[k][:], br_all[:, 0:1], None, ALU.add).then_inc(w_ready, 1)
                dve.wait_ge(w_ready, b + 1)
                assert ch.off == NA

            def place(b, k):
                ch = Chain(dve, b_step)
                ch.start(NB * b)
                dve.wait_ge(w_in, 16 * b + 16)
                for t in range(TT):
                    ch.mark(V.tensor_scalar(junk[:, 0:S], w_row[k][:], w_col[k][:, t:t + 1], 0.0, ALU.is_ge, ALU.add,
                                            accum_out=ge[:, t:t + 1])); ch.sync()
                    ch.mark(V.scalar_tensor_tensor(junk[:, 0:S], w_row[k][:], w_col[k][:, t:t + 1], later[:, t],
                                                   ALU.is_equal, ALU.mult, accum_out=eq[:, t:t + 1])); ch.sync()
                dve.wait_ge(slots_done, b + 1)
                V.tensor_tensor(rank[:], ge[:], eq[:], ALU.subtract)
                V.tensor_scalar(token[:, :, 0], token[:, :, 0], float(S), None, ALU.add)
                ch.mark(V.tensor_scalar(sel[:], ge[:], KSEL - 0.5, None, ALU.is_le)); ch.sync()
                for t in range(TT):
                    V.tensor_scalar(hot[:, t], slots_iota[:], rank[:, t:t + 1], None, ALU.is_equal)
                V.tensor_tensor(token[:, :, 1], sel[:], w_col[k][:], ALU.mult).then_inc(hot_ready, 1)
                dve.wait_ge(hot_ready, b + 1)
                ch.mark(V.tensor_scalar(base_f[:], sel[:], -1.0, 1.0, ALU.mult, ALU.add)); ch.sync()
                ch.mark(V.tensor_scalar(base_f[:], base_f[:], tg_f, None, ALU.mult)); ch.sync()
                for t in range(TT):
                    ins = V.scalar_tensor_tensor(x1t[k][:, t], xnt[k][:, t], base_f[:, t:t + 1], x1t[k][:, t],
                                                 ALU.mult, ALU.add)
                ins.then_inc(base_ready, 1)
                dve.wait_ge(base_ready, b + 1)
                dve.wait_ge(slots_done, b + 2)
                V.tensor_copy(slot_row[:, bass.ds(KT * b, KT)], s_ps[:, :, 0])
                ch.mark(V.tensor_scalar(slot_gate[:, bass.ds(KT * b, KT)], s_ps[:, :, 1], tg_f, None, ALU.mult)); ch.sync()
                dve.sem_inc(slots_read, 1)
                assert ch.off == NB

            dve.sem_inc(xn_out, 32)
            dve.sem_inc(slots_read, 1)
            dve.wait_ge(const_ready, 3)
            dve.wait_ge(wr_in, 32)
            batches(dve, weigh, place)

        @block.tensor
        def _(pe):
            T = nc.tensor

            def slots(b, k):
                pe.wait_ge(hot_ready, b + 1)
                pe.wait_ge(slots_read, b + 1)
                for j in range(KT):
                    for t in range(TT):
                        ins = T.matmul(s_ps[:, j, :], hot[:, t, j * P:(j + 1) * P], token[:, t, :],
                                       start=(t == 0), stop=(t == TT - 1))
                ins.then_inc(slots_done, 1)

            pe.sem_inc(slots_done, 1)
            batches(pe, lambda b, k: None, slots)


def experts(nc, v):
    L, DFF, SLOTS = v["L"], v["DFF"], v["SLOTS"]
    xn, outr, W1, b1, W2, b2 = (v[k] for k in ("xn", "outr", "W1", "b1", "W2", "b2"))
    ident, slot_row, slot_gate = v["ident"], v["slot_row"], v["slot_gate"]
    TOK = 4
    NT = TOK * P
    PASSES = SLOTS // TOK
    KT = L // P
    FT = 8
    GROUPS = DFF // (FT * P)
    DH = L // 512
    CH = TOK * DH
    TILES = PASSES * GROUPS * FT
    C_WOUT = 2
    with ExitStack() as c:
        def sb(n, s, d=F32): return c.enter_context(nc.sbuf_tensor(n, s, d))
        def sem(n): return c.enter_context(nc.semaphore(n))
        xTh, xTl = (sb(n, [P, KT, NT], F32R) for n in ("xTh", "xTl"))
        hh, hl = (sb(n, [P, FT, NT], F32R) for n in ("hh", "hl"))
        hf = [sb(f"hf{k}", [P, NT]) for k in range(2)]
        acc = sb("acc", [P, TOK, L])
        w1r = [sb(f"w1r{k}", [P, KT, P]) for k in range(2)]
        w1h = [sb(f"w1h{k}", [P, KT, P], F32R) for k in range(2)]
        w1l = [sb(f"w1l{k}", [P, KT, P], F32R) for k in range(2)]
        w2r = [sb(f"w2r{k}", [P, L]) for k in range(2)]
        w2h, w2l = (sb(n, [P, FT, L], F32R) for n in ("w2h", "w2l"))
        xg = sb("xg", [P, TOK, L])
        dl = [sb(f"dl{k}", [P, L]) for k in range(2)]
        b1c = sb("b1c", [P, DFF // P])
        get_row, put_row = sb("get_row", [P, TOK], I32), sb("put_row", [P, TOK], I32)
        h_ps = [c.enter_context(nc.psum_tensor(f"h_ps{k}", [P, NT], F32)) for k in range(2)]
        t_ps = [c.enter_context(nc.psum_tensor(f"xt_ps{k}", [P, NT], F32)) for k in range(2)]
        o_ps = [c.enter_context(nc.psum_tensor(f"o_ps{k}", [P, 512], F32)) for k in range(TOK)]

        bias_in = sem("bias_in")
        w1_in, w2_in = [sem(f"w1_in{k}") for k in range(2)], [sem(f"w2_in{k}") for k in range(2)]
        w1h_ready, w1l_ready, w2h_ready, w2l_ready = (sem(n) for n in ("w1h_ready", "w1l_ready", "w2h_ready", "w2l_ready"))
        h_done, gelu_done, hh_ready, hl_ready = (sem(n) for n in ("h_done", "gelu_done", "hh_ready", "hl_ready"))
        o_done, o_moved = sem("o_done"), sem("o_moved")
        rows_known, xg_in, turned, xh_ready, xl_ready = (sem(n) for n in ("rows_known", "xg_in", "xturned", "xh_ready", "xl_ready"))
        acc_ready, dl_ready, put = sem("acc_ready"), sem("dl_ready"), sem("put")
        dl_free = sem("dl_free")
        put_known, passed = sem("put_known"), sem("xpassed")
        block = c.enter_context(nc.Block())
        w1_view = W1.rearrange("(k p) f -> p k f", p=P)

        def passes(engine, begin, group):
            begin()
            with engine.Fori(0, PASSES - 1) as p:
                with engine.Fori(0, GROUPS - 1) as g:
                    group(p, g, False, True)
                group(p, GROUPS - 1, True, True)
            with engine.Fori(0, GROUPS - 1) as g:
                group(PASSES - 1, g, False, False)
            group(PASSES - 1, GROUPS - 1, True, False)

        @block.sync
        def _(sp):
            def load(F, k):
                f = F % (GROUPS * FT)
                sp.wait_ge(w1l_ready, C_WOUT + F - 1)
                sp.dma_start(w1r[k][:], w1_view[:, :, bass.ds(f * P, P)]).then_inc(w1_in[k], 16)
                sp.wait_ge(w2l_ready, C_WOUT + F - 1)
                sp.dma_start(w2r[k][:], W2[bass.ds(f * P, P), :]).then_inc(w2_in[k], 16)

            def group(p, g, last, more):
                for f in range(FT):
                    load((p * GROUPS + g) * FT + f + 1, (f + 1) % 2)

            with nc.allow_non_contiguous_dma("b1 by hidden unit"):
                sp.dma_start(b1c[:], b1.rearrange("(c p) -> p c", p=P)).then_inc(bias_in, 16)
            passes(sp, lambda: load(0, 0), group)
            sp.wait_ge(w1_in[0], 16 * (TILES // 2 + 1))
            sp.wait_ge(w2_in[0], 16 * (TILES // 2 + 1))

        @block.gpsimd
        def _(pool):
            G = nc.gpsimd

            def gather(p):
                G.tensor_copy(get_row[:], slot_row[:, bass.ds(p * TOK, TOK)]).then_inc(rows_known, 1)
                pool.wait_ge(rows_known, p + 1)
                settle(pool, passed)
                for q in range(TOK):
                    G.indirect_dma_start(out=xg[:, q, :], out_offset=None, in_=xn,
                                         in_offset=bass.IndirectOffsetOnAxis(ap=get_row[:, q:q + 1], axis=0)
                                         ).then_inc(xg_in, 16)

            def start_sums():
                G.dma_start(acc[:], bass.AP(b2.tensor, 0, [[0, P], [0, TOK], [1, L]])).then_inc(acc_ready, 16)

            def scatter(p):
                G.tensor_copy(put_row[:], slot_row[:, bass.ds(p * TOK, TOK)]).then_inc(put_known, 1)
                pool.wait_ge(put_known, p + 1)
                for q in range(TOK):
                    pool.wait_ge(dl_ready, TOK * p + q + 1)
                    settle(pool, passed)
                    G.indirect_dma_start(out=outr, out_offset=bass.IndirectOffsetOnAxis(ap=put_row[:, q:q + 1], axis=0),
                                         in_=dl[q % 2][:], in_offset=None, compute_op=ALU.add).then_inc(put, 16)
                    pool.wait_ge(put, 16 * (TOK * p + q + 1))
                    pool.sem_inc(dl_free, 1)

            def a_pass(p, more):
                if more:
                    pool.wait_ge(turned, KT * (p + 1) + 2)
                    gather(p + 1)
                scatter(p)
                if more:
                    start_sums()

            pool.sem_inc(dl_free, 2)
            gather(0)
            start_sums()
            with pool.Fori(0, PASSES - 1) as p:
                a_pass(p, True)
            a_pass(PASSES - 1, False)

        @block.scalar
        def _(act):
            A = nc.scalar

            def split_w1(F, k):
                act.wait_ge(w1_in[k], 16 * (F // 2) + 16)
                act.wait_ge(h_done, C_WOUT + F - 1)
                A.activation(w1h[k][:], w1r[k][:], ACT.Copy).then_inc(w1h_ready, 1)

            def turn_high(p, k):
                act.wait_ge(turned, KT * p + k + 1 + 2)
                A.activation(xTh[:, k, :], t_ps[k % 2][:], ACT.Copy).then_inc(xh_ready, 1)

            def begin():
                for k in range(KT):
                    turn_high(0, k)
                split_w1(0, 0)

            def group(p, g, last, more):
                n = p * GROUPS + g
                for f in range(FT):
                    F = n * FT + f
                    split_w1(F + 1, (f + 1) % 2)
                    act.wait_ge(w2_in[f % 2], 16 * (F // 2) + 16)
                    if f == 0:
                        act.wait_ge(o_done, CH * n + TOK)
                    A.activation(w2h[:, f, :], w2r[f % 2][:], ACT.Copy).then_inc(w2h_ready, 1)
                    act.wait_ge(h_done, C_WOUT + F + 1)
                    act.wait_ge(hl_ready, C_WOUT + F - 1)
                    A.activation(hf[f % 2][:], h_ps[f % 2][:], ACT.Gelu_apprx_tanh,
                                 bias=b1c[:, bass.ds(g * FT + f, 1)]).then_inc(gelu_done, 1)
                    act.wait_ge(gelu_done, 2 + F + 1)
                    A.activation(hh[:, f, :], hf[f % 2][:], ACT.Copy).then_inc(hh_ready, 1)
                if last and more:
                    for k in range(KT):
                        turn_high(p + 1, k)

            act.wait_ge(bias_in, 16)
            passes(act, begin, group)

        @block.vector
        def _(dve):
            V = nc.vector

            def split_w1(F, k):
                dve.wait_ge(w1h_ready, F + 1)
                V.tensor_tensor(w1l[k][:], w1r[k][:], w1h[k][:].bitcast(F32), ALU.subtract).then_inc(w1l_ready, 1)

            def turn_low(p, k):
                dve.wait_ge(xh_ready, KT * p + k + 1)
                V.tensor_tensor(xTl[:, k, :], t_ps[k % 2][:], xTh[:, k, :].bitcast(F32), ALU.subtract).then_inc(xl_ready, 1)

            def begin():
                for k in range(KT):
                    turn_low(0, k)
                split_w1(0, 0)

            def group(p, g, last, more):
                n = p * GROUPS + g
                for f in range(FT):
                    F = n * FT + f
                    split_w1(F + 1, (f + 1) % 2)
                    dve.wait_ge(w2h_ready, F + 1)
                    V.tensor_tensor(w2l[:, f, :], w2r[f % 2][:], w2h[:, f, :].bitcast(F32), ALU.subtract).then_inc(w2l_ready, 1)
                    dve.wait_ge(hh_ready, F + 1)
                    V.tensor_tensor(hl[:, f, :], hf[f % 2][:], hh[:, f, :].bitcast(F32), ALU.subtract).then_inc(hl_ready, 1)
                dve.wait_ge(acc_ready, 16 * p + 16)
                turns = last and more
                for i in range(CH):
                    if turns and i == 0:
                        for k in range(TOK):
                            turn_low(p + 1, k)
                    a = acc[:, i % TOK, (i // TOK) * 512:(i // TOK + 1) * 512]
                    dve.wait_ge(o_done, TOK + CH * n + i + 1)
                    V.tensor_tensor(a, a, o_ps[i % TOK][:], ALU.add).then_inc(o_moved, 1)
                    if turns and i >= TOK:
                        turn_low(p + 1, i)
                dve.wait_ge(o_moved, TOK + CH * (n + 1))
                if last:
                    for q in range(TOK):
                        dve.wait_ge(dl_free, TOK * p + q + 1)
                        V.tensor_scalar(dl[q % 2][:], acc[:, q, :], slot_gate[:, bass.ds(p * TOK + q, 1)], None,
                                        ALU.mult).then_inc(dl_ready, 1)

            passes(dve, begin, group)

        @block.tensor
        def _(pe):
            T = nc.tensor

            def turn(p, k):
                if k == 0:
                    pe.wait_ge(xg_in, 16 * TOK * (p + 1))
                pe.wait_ge(xl_ready, KT * p + k + 1)
                for q in range(TOK):
                    ins = T.transpose(t_ps[k % 2][:, q * P:(q + 1) * P], xg[:, q, k * P:(k + 1) * P], ident[:])
                ins.then_inc(turned, 1)

            def begin():
                for k in range(KT):
                    turn(0, k)

            def hidden(F, k):
                pe.wait_ge(w1l_ready, C_WOUT + F + 1)
                pe.wait_ge(gelu_done, 2 + F - 1)
                for kt in range(KT):
                    for j, (w, xx) in enumerate(((w1h, xTh), (w1h, xTl), (w1l, xTh))):
                        ins = T.matmul(h_ps[k][:], w[k][:, kt, :], xx[:, kt, :], start=(kt == 0 and j == 0),
                                       stop=(kt == KT - 1 and j == 2))
                ins.then_inc(h_done, 1)

            def down(i, fs, start, stop):
                q, d = i % TOK, i // TOK
                for f in fs:
                    for j, (ha, w) in enumerate(((hh, w2h), (hh, w2l), (hl, w2h))):
                        ins = T.matmul(o_ps[q][:], ha[:, f, q * P:(q + 1) * P], w[:, f, d * 512:(d + 1) * 512],
                                       start=(start and f == 0 and j == 0), stop=(stop and f == FT - 1 and j == 2))
                return ins

            def group(p, g, last, more):
                n = p * GROUPS + g
                pe.wait_ge(xl_ready, KT * (p + 1) + 2)
                for f in range(FT):
                    hidden(n * FT + f, f % 2)
                pe.wait_ge(hl_ready, C_WOUT + (n + 1) * FT - 1)
                pe.wait_ge(w2l_ready, C_WOUT + (n + 1) * FT - 1)
                for i in range(TOK):
                    pe.wait_ge(o_moved, CH * n + i + 1)
                    down(i, range(FT - 1), True, False)
                    if last and more:
                        turn(p + 1, i)
                pe.wait_ge(hl_ready, C_WOUT + (n + 1) * FT)
                pe.wait_ge(w2l_ready, C_WOUT + (n + 1) * FT)
                for i in range(TOK):
                    down(i, [FT - 1], False, True).then_inc(o_done, 1)
                for i in range(TOK, CH):
                    pe.wait_ge(o_moved, CH * n + i + 1)
                    down(i, range(FT), True, True).then_inc(o_done, 1)
                    if last and more:
                        turn(p + 1, i)

            pe.sem_inc(xl_ready, 2)
            pe.sem_inc(turned, 2)
            pe.sem_inc(h_done, C_WOUT)
            pe.sem_inc(o_done, TOK)
            pe.sem_inc(o_moved, TOK)
            pe.sem_inc(gelu_done, 2)
            pe.sem_inc(hl_ready, C_WOUT)
            pe.sem_inc(w1l_ready, C_WOUT)
            pe.sem_inc(w2l_ready, C_WOUT)
            passes(pe, begin, group)


_INS = ["x", "ctx_2048", "g_xattn", "g_ffn", "L0_xattn_ssm_kernel", "L0_xattn_D", "L0_ffn_W_r", "L0_ffn_b_r",
        "L0_ffn_W1", "L0_ffn_b1", "L0_ffn_W2", "L0_ffn_b2"]


def kernel(**inputs):
    import numpy as _np
    import concourse.bacc as _bacc
    from concourse import mybir as _mybir
    from concourse.bass_utils import run_bass_kernel_spmd as _run

    nc = _bacc.Bacc("TRN2", target_bir_lowering=False, num_devices=1)
    arrays, args = {}, []
    for name in _INS:
        a = _np.ascontiguousarray(inputs[name])
        arrays[f"in_{name}_dram"] = a
        args.append(nc.dram_tensor(f"in_{name}_dram", a.shape, _mybir.dt.from_np(a.dtype), kind="ExternalInput").ap())
    out = nc.dram_tensor("out_dram", inputs["x"].shape, _mybir.dt.float32, kind="ExternalOutput").ap()
    build(nc, *args, out)
    return _run(nc, [arrays], core_ids=[0]).results[0]["out_dram"]
```

```python
from contextlib import ExitStack

import concourse.bass as bass
from concourse import mybir

F32, F32R, F16, I32 = mybir.dt.float32, mybir.dt.float32r, mybir.dt.float16, mybir.dt.int32
ALU = mybir.AluOpType
ACT = mybir.ActivationFunctionType
AX_X = mybir.AxisListType.X
P = 128
EXPONENT = 0x7F800000
TINY = 1e-30
EPS = 1e-5


class Chain:

    def __init__(self, engine, sem):
        self.engine, self.sem, self.base, self.off = engine, sem, 0, 0

    def start(self, base):
        self.base, self.off = base, 0

    def mark(self, instruction):
        instruction.then_inc(self.sem, 1)
        self.off += 1
        return self.off

    def sync(self):
        self.engine.wait_ge(self.sem, self.base + self.off)


def settle(engine, passed):
    engine.sem_inc(passed, 1)


def build(nc, x, ctx, g_xattn, g_ffn, kern, D, W_r, b_r, W1, b1, W2, b2, out):
    B, S, L = x.shape
    H = kern.shape[0]
    HD = S // H
    GR = P // HD
    NG = H // GR
    BH = B // 2
    NL = L // P
    PAIRS = HD * (HD + 1) // 2
    COLS = BH * PAIRS
    LB = NL * BH
    HALF = NL // 2
    STAGES = 2 * NG
    PADK = P + L
    DFF = W1.shape[1]
    KSEL = 256
    TT = S // P
    SLOTS = B * KSEL // P

    kpad = nc.dram_tensor("kpad", [2, H, PADK], F16).ap()
    kinv = nc.dram_tensor("kinv", [H, HD], F32).ap()
    x1 = nc.dram_tensor("x1", [B * S, L], F32).ap()
    wall = nc.dram_tensor("wall", [B, S], F32).ap()
    xr = x.rearrange("b s l -> (b s) l")
    cr = ctx.rearrange("b s l -> (b s) l")
    outr = out.rearrange("b s l -> (b s) l")

    top = ExitStack()
    with top:
        ident = top.enter_context(nc.sbuf_tensor("ident", [P, P], F32))
        gates = top.enter_context(nc.sbuf_tensor("gates", [P, 4], F32))
        kinv_col = top.enter_context(nc.sbuf_tensor("kinv_col", [P, NG], F32))
        tg_x, tg_f = gates[:, 2:3], gates[:, 3:4]
        setup(nc, H, L, HD, PADK, NG, kern, D, g_xattn, g_ffn, kpad, kinv, ident, gates, kinv_col)
        conv(nc, locals())
        experts(nc, locals())


def setup(nc, H, L, HD, PADK, NG, kern, D, g_xattn, g_ffn, kpad, kinv, ident, gates, kinv_col):
    with ExitStack() as c:
        def sb(n, s, d): return c.enter_context(nc.sbuf_tensor(n, s, d))
        def sem(n): return c.enter_context(nc.semaphore(n))
        K = sb("K", [H, L], F32)
        Ks = sb("Ks", [H, L], F32)
        Dc = sb("Dc", [H, 1], F32)
        Kh = sb("Kh", [H, PADK], F16)
        Kl = sb("Kl", [H, PADK], F16)
        m = sb("km", [H, 4], F32)
        inv8 = sb("inv8", [H, HD], F32)
        inputs_in, gates_in = sem("inputs_in"), sem("gates_in")
        step, ident_ready = sem("setup_step"), sem("ident_ready")
        parts_ready, parts_out, inv_in = sem("parts_ready"), sem("parts_out"), sem("inv_in")
        tanh_done = sem("tanh_done")
        block = c.enter_context(nc.Block())

        @block.sync
        def _(sp):
            sp.dma_start(K[:], kern).then_inc(inputs_in, 16)
            sp.dma_start(Dc[:], D.rearrange("(h a) -> h a", a=1)).then_inc(inputs_in, 16)
            sp.dma_start(gates[:, 0:1], bass.AP(g_xattn.tensor, 0, [[0, P], [1, 1]])).then_inc(gates_in, 16)
            sp.dma_start(gates[:, 1:2], bass.AP(g_ffn.tensor, 0, [[0, P], [1, 1]])).then_inc(gates_in, 16)
            sp.wait_ge(parts_ready, 1)
            sp.dma_start(kpad[0], Kh[:]).then_inc(parts_out, 16)
            sp.dma_start(kpad[1], Kl[:]).then_inc(parts_out, 16)
            sp.dma_start(kinv, inv8[:]).then_inc(parts_out, 16)
            sp.wait_ge(parts_out, 48)
            with nc.allow_non_contiguous_dma("a few words"):
                sp.dma_start(kinv_col[:], bass.AP(kinv.tensor, 0, [[1, P], [P, NG]])).then_inc(inv_in, 16)
            sp.wait_ge(inv_in, 16)

        @block.scalar
        def _(act):
            act.wait_ge(gates_in, 32)
            nc.scalar.activation(gates[:, 2:4], gates[:, 0:2], ACT.Tanh).then_inc(tanh_done, 1)

        @block.gpsimd
        def _(pool):
            nc.gpsimd.memset(ident[:], 0.0).then_inc(ident_ready, 1)
            pool.wait_ge(ident_ready, 1)
            nc.gpsimd.affine_select(out=ident[:], in_=ident[:], compare_op=ALU.not_equal, fill=1.0, base=0,
                                    pattern=[[-1, P]], channel_multiplier=1).then_inc(ident_ready, 1)

        @block.vector
        def _(dve):
            ch = Chain(dve, step)
            V = nc.vector
            ch.mark(V.memset(Kh[:, 0:P], 0.0))
            ch.mark(V.memset(Kl[:, 0:P], 0.0))
            dve.wait_ge(inputs_in, 32)
            ch.mark(V.tensor_tensor(K[:, 0:1], K[:, 0:1], Dc[:], ALU.add)); ch.sync()
            ch.mark(V.tensor_reduce(m[:, 0:1], K[:], AX_X, ALU.max, apply_absolute_value=True)); ch.sync()
            ch.mark(V.tensor_scalar(m[:, 1:2], m[:, 0:1], TINY, None, ALU.max)); ch.sync()
            ch.mark(V.tensor_scalar(m[:, 2:3].bitcast(I32), m[:, 1:2].bitcast(I32), EXPONENT, None,
                                    ALU.bitwise_and)); ch.sync()
            ch.mark(V.reciprocal(m[:, 3:4], m[:, 2:3])); ch.sync()
            ch.mark(V.tensor_scalar(Ks[:], K[:], m[:, 3:4], 8192.0, ALU.mult, ALU.mult)); ch.sync()
            ch.mark(V.tensor_copy(Kh[:, P:PADK], Ks[:])); ch.sync()
            ch.mark(V.tensor_tensor(Kl[:, P:PADK], Ks[:], Kh[:, P:PADK], ALU.subtract))
            ch.mark(V.memset(inv8[:], 1.0 / 8192.0)); ch.sync()
            V.tensor_scalar(inv8[:], inv8[:], m[:, 2:3], None, ALU.mult).then_inc(parts_ready, 1)


def conv(nc, v):
    B, S, L, H, HD, GR, NG, BH, NL = (v[k] for k in ("B", "S", "L", "H", "HD", "GR", "NG", "BH", "NL"))
    PAIRS, COLS, HALF, STAGES, PADK = (v[k] for k in ("PAIRS", "COLS", "HALF", "STAGES", "PADK"))
    kpad, x1, xr, cr = (v[k] for k in ("kpad", "x1", "xr", "cr"))
    ident, kinv_col, tg_x = v["ident"], v["kinv_col"], v["tg_x"]
    HLB = HALF * BH
    QLB = HLB // 2
    FULL = HD // 2
    WRAP = HD + FULL - 1
    assert PAIRS == FULL * HD + FULL
    LB = NL * BH
    YB = 4
    UP = GR // 2
    assert UP == BH
    C_TURNED, C_MOVED, C_DONE, C_YMOVED, C_TERMS, C_LOW, C_BACK, C_KV, C_OUT = 4, 2, 2 * NL, YB, 4, 2, 2, 2, 2
    with ExitStack() as c:
        def sb(n, s, d): return c.enter_context(nc.sbuf_tensor(n, s, d))
        def pb(n, s): return c.enter_context(nc.psum_tensor(n, s, F32))
        def sem(n): return c.enter_context(nc.semaphore(n))
        ctxT_all = sb("ctxT", [P, 2, NL, BH, P], F32)
        ctxT = [ctxT_all[:, k] for k in range(2)]
        qT = [sb(f"qT{k}", [P, NL, BH, P], F32) for k in range(2)]
        kv = [sb(f"kv{k}", [P, HALF, BH, PAIRS], F32) for k in range(2)]
        kvh = [sb(f"kvh{k}", [P, NL, BH, PAIRS], F16) for k in range(2)]
        kvl = [sb(f"kvl{k}", [P, NL, BH, PAIRS], F16) for k in range(2)]
        y = [sb(f"y{k}", [P, HALF, BH, PAIRS], F32) for k in range(2)]
        cx = [sb(f"cx{k}", [P, HLB, WRAP], F32) for k in range(2)]
        qx = [sb(f"qx{k}", [P, HLB, WRAP], F32) for k in range(2)]
        prod = [sb(f"prod{k}", [P, QLB, HD * HD], F32) for k in range(2)]
        toep = [sb(f"toep{k}", [P, 2, L], F16) for k in range(2)]
        c_row = sb("c_row", [P, L], F32)
        x_row = sb("x_row", [P, L], F32)
        s_row = sb("s_row", [P, L], F32)
        f_row = sb("f_row", [P, L], F32)
        staged = sb("staged", [P, NL, P], F32)
        coef = sb("coef", [P, 3, BH], F32)
        st = sb("st", [P, 2, 6], F32)
        sc = sb("sc", [P, 12], F32)
        y_ps = [pb(f"y_ps{k}", [P, 512]) for k in range(YB)]
        t_ps = [pb(f"t_ps{k}", [P, 4, P]) for k in range(2)]
        f_ps = [pb(f"f_ps{k}", [P, 4, P]) for k in range(2)]

        ctx_in, x_in, fx_in, x1_out = sem("ctx_in"), sem("x_in"), sem("fx_in"), sem("x1_out")
        passed = sem("passed")
        toep_in = [sem(f"toep_in{k}") for k in range(2)]
        sum_step, prep_step = sem("sum_step"), sem("prep_step")
        var_ready, std_ready = sem("var_ready"), sem("std_ready")
        cs_ready, q_ready = sem("cs_ready"), sem("q_ready")
        cx_ready, cscale_ready, qscale_ready = sem("cx_ready"), sem("cscale_ready"), sem("qscale_ready")
        turned, turned_moved = sem("turned"), sem("turned_moved")
        kv_ready, kvh_ready, kvl_ready = sem("kv_ready"), sem("kvh_ready"), sem("kvl_ready")
        y_done, y_moved = sem("y_done"), sem("y_moved")
        terms_made = sem("terms_made")
        out_ready, staged_ready, back, x1_ready = sem("out_ready"), sem("staged_ready"), sem("back"), sem("x1_ready")
        block = c.enter_context(nc.Block())

        def stages(engine, step, prepare, finish, begin=None):
            if prepare:
                with engine.Fori(0, UP) as u:
                    prepare(0, 0, u)
            if begin:
                begin()
            with engine.Fori(0, UP) as u:
                step(0, 0, u, False, True, True)
            with engine.Fori(0, (STAGES - 2) // 2) as sp:
                for k in range(2):
                    with engine.Fori(0, UP) as u:
                        step(2 * sp + (1 + k), (k + 1) % 2, u, True, True, True)
            with engine.Fori(0, UP - 1) as u:
                step(STAGES - 1, (STAGES - 1) % 2, u, True, False, True)
            step(STAGES - 1, (STAGES - 1) % 2, UP - 1, True, False, False)
            if finish:
                with engine.Fori(0, UP) as u:
                    finish(STAGES, STAGES % 2, u)

        def slide(t, shape, first=0):
            whole = t[:]
            step = whole.ap[0][0]
            return bass.AP(whole.tensor, whole.offset + first * WRAP, [[step, P], [WRAP, shape[1]], [1, shape[2]], [1, shape[3]]])

        def rows(t, s, u):
            first = ((s // NG) * BH + u) * S + (s % NG) * P
            return t[bass.ds(first, P), :]

        @block.sync
        def _(sp):
            def load(m):
                sp.wait_ge(cs_ready, m + 1)
                sp.dma_start(c_row[:], rows(cr, (m // UP) % STAGES, m % UP)).then_inc(ctx_in, 16)
                sp.wait_ge(q_ready, m + 1)
                sp.dma_start(x_row[:], rows(xr, (m // UP) % STAGES, m % UP)).then_inc(x_in, 16)

            def kernels(n, k):
                h = ((n // GR) % NG) * GR + n % GR
                for part in range(2):
                    src = bass.AP(kpad.tensor, (h + part * H) * PADK + 1, [[1, P], [1, L]])
                    sp.dma_start(toep[k][:, part, :], src).then_inc(toep_in[k], 16)

            def fetch(s, par, u):
                n = (s - 1) * UP + u
                sp.wait_ge(x1_out, 16 * n + 16)
                sp.dma_start(f_row[:], rows(xr, s - 1, u)).then_inc(fx_in, 16)

            def store(s, par, u):
                n = (s - 1) * UP + u
                sp.wait_ge(x1_ready, 1 + n + 1)
                sp.dma_start(rows(x1, s - 1, u), f_row[:]).then_inc(x1_out, 16)

            def step(s, par, u, fin, prep, more):
                if fin:
                    fetch(s, par, u)
                for k in range(2):
                    n = s * GR + 2 * u + k
                    if more:
                        sp.wait_ge(y_done, C_DONE + NL * n + NL)
                        kernels(n + 2, k)
                    if k == 0 and prep:
                        load((s + 1) * UP + u + 1)
                if fin:
                    store(s, par, u)

            def last(s, par, u):
                fetch(s, par, u)
                store(s, par, u)

            def begin():
                load(UP)
                kernels(0, 0)
                kernels(1, 1)

            sp.sem_inc(x1_out, 16)
            stages(sp, step, lambda s, par, u: load(u), last, begin)
            sp.wait_ge(x1_out, 16 * STAGES * UP + 16)

        @block.gpsimd
        def _(pool):
            G = nc.gpsimd

            def step(s, par, u, fin, prep, more):
                for k in range(2):
                    n = s * GR + 2 * u + k

                    def products(half):
                        pool.wait_ge(cx_ready, 2 * n + half + 1)
                        pool.wait_ge(kvl_ready, C_LOW + 2 * n + half - 1)
                        dst = kv[half][:].rearrange("p a b r -> p (a b) r")
                        both = [P, HLB, FULL, HD]
                        G.tensor_tensor(dst[:, :, 0:FULL * HD].rearrange("p a (d i) -> p a d i", d=FULL),
                                        cx[half][:, :, 0:HD].rearrange("p a (d i) -> p a d i", d=1).broadcast_to(both),
                                        slide(cx[half], both), ALU.mult)
                        G.tensor_tensor(dst[:, :, FULL * HD:PAIRS], cx[half][:, :, 0:FULL], cx[half][:, :, FULL:HD],
                                        ALU.mult).then_inc(kv_ready, 1)

                    def low(half):
                        pool.wait_ge(kvh_ready, 2 * n + half + 1)
                        a = slice(half * HALF, (half + 1) * HALF)
                        G.tensor_tensor(kvl[k][:, a], kv[half][:], kvh[k][:, a], ALU.subtract).then_inc(kvl_ready, 1)

                    products(0)
                    products(1)
                    pool.wait_ge(y_done, C_DONE + NL * n - NL)
                    low(0)
                    low(1)

            pool.sem_inc(kvl_ready, C_LOW)
            pool.sem_inc(kv_ready, C_KV)
            stages(pool, step, None, None)

        @block.scalar
        def _(act):
            A = nc.scalar

            def root(m):
                act.wait_ge(var_ready, m + 1)
                A.activation(sc[:, 6:7], sc[:, 5:6], ACT.Sqrt).then_inc(std_ready, 1)

            def scale_ctx(m):
                act.wait_ge(cscale_ready, m + 1)
                act.wait_ge(turned, C_TURNED + 4 * m)
                A.activation(s_row[:, ::-1], c_row[:], ACT.Copy, scale=sc[:, 3:4]).then_inc(cs_ready, 1)

            def scale_x(m):
                act.wait_ge(qscale_ready, m + 1)
                act.wait_ge(turned, C_TURNED + 4 * m + 2)
                A.activation(s_row[:], x_row[:], ACT.Identity, bias=sc[:, 10:11], scale=sc[:, 9:10]).then_inc(q_ready, 1)

            def turn(s, par, u, groups):
                n = s * UP + u
                for g in groups:
                    dst = (ctxT if g < 2 else qT)[par]
                    a = (g % 2) * 4
                    act.wait_ge(turned, C_TURNED + 4 * n + g + 1)
                    settle(act, passed)
                    A.activation(dst[:, a:a + 4, bass.ds(u, 1), :].rearrange("p a b r -> p a (b r)"), t_ps[g % 2][:],
                                 ACT.Copy).then_inc(turned_moved, 1)

            def prepare(s, par, u):
                turn(s, par, u, range(2))
                scale_x(s * UP + u)
                turn(s, par, u, range(2, 4))
                root(s * UP + u + 1)
                scale_ctx(s * UP + u + 1)

            def stage_out(s, par, u):
                n = (s - 1) * UP + u
                act.wait_ge(out_ready, C_OUT + 4 * GR * s)
                act.wait_ge(back, C_BACK + 2 * n)
                A.activation(staged[:], qT[1 - par][:, :, bass.ds(u, 1), :].rearrange("p a b r -> p a (b r)"),
                             ACT.Copy).then_inc(staged_ready, 1)

            def lay(dst, src, half, col):
                part = src[:, half * HALF:(half + 1) * HALF].rearrange("p a b r -> p (a b) r")
                A.activation(dst[half][:, :, 0:HD], part[:, :, bass.ds(col, HD)], ACT.Copy)
                return A.activation(dst[half][:, :, HD:WRAP], part[:, :, bass.ds(col, WRAP - HD)], ACT.Copy)

            def lay_ctx(n):
                first = ((n // GR) % 2) * (LB * P) + (n % GR) * HD
                for half in range(2):
                    act.wait_ge(kv_ready, C_KV + 2 * n + half - 1)
                    src = [bass.AP(ctxT_all[:].tensor, first + half * HLB * P, [[2 * LB * P, P], [P, HLB], [1, w]])
                           for w in (HD, WRAP - HD)]
                    A.activation(cx[half][:, :, 0:HD], src[0], ACT.Copy)
                    A.activation(cx[half][:, :, HD:WRAP], src[1], ACT.Copy).then_inc(cx_ready, 1)

            def high(n, k, half):
                if half == 0:
                    act.wait_ge(y_done, C_DONE + NL * n - NL)
                act.wait_ge(kv_ready, C_KV + 2 * n + half + 1)
                A.activation(kvh[k][:, half * HALF:(half + 1) * HALF], kv[half][:],
                             ACT.Copy).then_inc(kvh_ready, 1)

            def begin():
                act.wait_ge(turned_moved, C_MOVED + 4 * UP)
                lay_ctx(0)
                lay_ctx(1)
                high(0, 0, 0)
                high(0, 0, 1)

            def step(s, par, u, fin, prep, more):
                act.wait_ge(turned_moved, C_MOVED + 4 * UP * (s + 1))
                for k in range(2):
                    n = s * GR + 2 * u + k
                    for lt in range(NL):
                        half, a = lt // HALF, lt % HALF
                        if a == 0:
                            act.wait_ge(terms_made, C_TERMS + 4 * n + 2 * half - 2)
                            lay(qx, qT[par], half, (2 * u + k) * HD)
                        act.wait_ge(y_done, C_DONE + NL * n + lt + 1)
                        A.activation(y[half][:, a].rearrange("p b r -> p (b r)"), y_ps[lt % YB][:, 0:COLS],
                                     ACT.Copy).then_inc(y_moved, 1)
                        m = (s + 1) * UP + u
                        if lt == 3 and prep:
                            if k == 1 and fin:
                                act.wait_ge(staged_ready, (s - 1) * UP + u + 1)
                            turn(s + 1, 1 - par, u, range(2 * k, 2 * k + 2))
                        if lt in (3, 5) and (more or k == 0):
                            high(n + 1, 1 - k, lt // 4)
                        if lt == 5 and k == 0 and prep:
                            scale_x(m)
                        if lt == 6 and more:
                            if prep:
                                act.wait_ge(turned_moved, C_MOVED + 4 * UP * (s + 1) + 4 * u + 2)
                            lay_ctx(n + 2)
                    if k == 0 and fin:
                        stage_out(s, par, u)
                    if k == 1 and prep:
                        root(m + 1)
                        scale_ctx(m + 1)

            act.sem_inc(turned_moved, C_MOVED)
            act.sem_inc(y_moved, C_YMOVED)
            act.sem_inc(cs_ready, 1)
            act.sem_inc(q_ready, 1)
            root(0)
            scale_ctx(0)
            stages(act, step, prepare, stage_out, begin)

        @block.vector
        def _(dve):
            V = nc.vector

            def diagonal(t, first, rows, width):
                whole = t[:]
                return bass.AP(whole.tensor, whole.offset + first,
                               [[whole.ap[0][0], P], [HD * HD, QLB], [HD + 1, rows], [1, width]])

            def quarter(n, r, par, col, make, add, beside=()):
                Q = 4 * n + r
                half, t, b = r // 2, prod[r % 2], prod[(r - 1) % 2]
                a = slice((r % 2) * QLB, (r % 2 + 1) * QLB)
                both = [P, QLB, FULL, HD]
                small = iter(beside)

                def other():
                    for f in small:
                        f()
                        break

                if make:
                    q = qx[half][:, a]
                    ys = y[half][:].rearrange("p a b r -> p (a b) r")[:, a]
                    yd = ys[:, :, 0:FULL * HD].rearrange("p a (d i) -> p a d i", d=FULL)
                    if r % 2 == 0:
                        dve.wait_ge(y_moved, C_YMOVED + NL * n + HALF * (half + 1))
                    dve.wait_ge(out_ready, C_OUT + Q - 1)
                    V.tensor_tensor(t[:, :, 0:FULL * HD].rearrange("p a (d i) -> p a d i", d=FULL), yd,
                                    slide(qx[half], both, (r % 2) * QLB), ALU.mult)
                    other()
                if add:
                    dve.wait_ge(terms_made, C_TERMS + Q)
                    V.tensor_tensor(b[:, :, 0:32], b[:, :, 0:32], b[:, :, 32:64], ALU.add).then_inc(sum_step, 1)
                    other()
                if make:
                    V.tensor_tensor(diagonal(t, FULL * HD + 1, FULL - 1, HD), yd[:, :, 1:FULL],
                                    q[:, :, 0:HD].rearrange("p a (d i) -> p a d i", d=1)
                                    .broadcast_to([P, QLB, FULL - 1, HD]), ALU.mult)
                    other()
                if add:
                    dve.wait_ge(sum_step, 2 * Q - 1)
                    V.tensor_tensor(b[:, :, 0:16], b[:, :, 0:16], b[:, :, 16:32], ALU.add).then_inc(sum_step, 1)
                    other()
                if make:
                    V.tensor_tensor(t[:, :, HD * HD - FULL:HD * HD], ys[:, :, FULL * HD:PAIRS], q[:, :, 0:FULL], ALU.mult)
                    V.tensor_tensor(diagonal(t, FULL * HD, FULL, 1),
                                    ys[:, :, FULL * HD:PAIRS].rearrange("p a (d i) -> p a d i", i=1),
                                    q[:, :, FULL:HD].rearrange("p a (d i) -> p a d i", i=1), ALU.mult).then_inc(terms_made, 1)
                    other()
                if add:
                    dve.wait_ge(sum_step, 2 * Q)
                    lt = 2 * (r - 1)
                    o = qT[par][:, lt:lt + 2].rearrange("p a b r -> p (a b) r")
                    V.tensor_tensor(o[:, :, bass.ds(col, HD)], b[:, :, 0:HD], b[:, :, HD:2 * HD], ALU.add).then_inc(out_ready, 1)
                    other()

            ch = Chain(dve, prep_step)

            def ctx_in_steps(m):
                def largest():
                    ch.start(10 * m + 10)
                    ch.sync()
                    dve.wait_ge(ctx_in, 16 * m + 16)
                    dve.wait_ge(cs_ready, m + 1)
                    ch.mark(V.tensor_reduce(sc[:, 0:1], c_row[:], AX_X, ALU.max, apply_absolute_value=True))

                def above_zero():
                    ch.sync()
                    ch.mark(V.tensor_scalar(sc[:, 1:2], sc[:, 0:1], TINY, 1.0 / 64, ALU.max, ALU.mult))

                def power_of_two():
                    ch.sync()
                    ch.mark(V.tensor_scalar(sc[:, 2:3].bitcast(I32), sc[:, 1:2].bitcast(I32), EXPONENT, None,
                                            ALU.bitwise_and))

                def inverse():
                    ch.sync()
                    V.reciprocal(sc[:, 3:4], sc[:, 2:3]).then_inc(cscale_ready, 1)

                return largest, above_zero, power_of_two, inverse

            def x_in_steps(m):
                def first_half():
                    dve.wait_ge(x_in, 16 * m + 16)
                    V.bn_stats(st[:, 0, :], x_row[:, 0:512])

                def second_half():
                    ch.mark(V.bn_stats(st[:, 1, :], x_row[:, 512:1024]))

                def both_halves():
                    ch.sync(); settle(dve, passed)
                    ch.mark(V.bn_aggr(sc[:, 4:6], st[:].rearrange("p a b -> p (a b)")))

                def variance():
                    ch.sync()
                    V.tensor_scalar(sc[:, 5:6], sc[:, 5:6], EPS, None, ALU.add).then_inc(var_ready, 1)

                return first_half, second_half, both_halves, variance

            def factor_steps(m):
                def inverse():
                    dve.wait_ge(std_ready, m + 1)
                    dve.wait_ge(q_ready, m + 1)
                    ch.mark(V.reciprocal(sc[:, 6:7], sc[:, 6:7]))

                def square():
                    ch.sync()
                    ch.mark(V.tensor_scalar(sc[:, 7:8], sc[:, 6:7], sc[:, 6:7], sc[:, 5:6], ALU.mult, ALU.mult))

                def correction():
                    ch.sync()
                    ch.mark(V.tensor_scalar(sc[:, 8:9], sc[:, 7:8], -0.5, 1.5, ALU.mult, ALU.add))

                def factor():
                    ch.sync()
                    ch.mark(V.tensor_scalar(sc[:, 9:10], sc[:, 8:9], sc[:, 6:7], sc[:, 2:3], ALU.mult, ALU.mult))

                def shift():
                    ch.sync()
                    V.tensor_scalar(sc[:, 10:11], sc[:, 9:10], sc[:, 4:5], -1.0, ALU.mult, ALU.mult).then_inc(qscale_ready, 1)

                def scale_back():
                    ch.mark(V.tensor_scalar(coef[:, bass.ds((m // UP) % 3, 1), bass.ds(m % UP, 1)].rearrange("p a b -> p (a b)"),
                                            kinv_col[:, bass.ds((m // UP) % NG, 1)], sc[:, 2:3], None, ALU.mult))
                    assert ch.off == 10

                return inverse, square, correction, factor, shift, scale_back

            def prepare_rows(m):
                for f in ctx_in_steps(m) + x_in_steps(m) + factor_steps(m):
                    f()

            def prepare(s, par, u):
                prepare_rows(s * UP + u + 1)

            def finish_steps(s, u):
                n = (s - 1) * UP + u

                def bank(g):
                    a = slice(512 * g, 512 * (g + 1))
                    return V.scalar_tensor_tensor(f_row[:, a], f_ps[g][:].rearrange("p a b -> p (a b)"),
                                                  coef[:, bass.ds((s - 1) % 3, 1), bass.ds(u, 1)].rearrange("p a b -> p (a b)"),
                                                  f_row[:, a], ALU.mult, ALU.add)

                def first():
                    dve.wait_ge(x1_ready, 1 + n)
                    dve.wait_ge(fx_in, 16 * n + 16)
                    dve.wait_ge(back, C_BACK + 2 * n + 2)
                    bank(0)

                def second():
                    bank(1).then_inc(x1_ready, 1)

                return first, second

            def finish(s, par, u):
                for f in finish_steps(s, u):
                    f()

            def step(s, par, u, fin, prep, more):
                m = (s + 1) * UP + u + 1
                none = ()
                c, x, f = (ctx_in_steps(m), x_in_steps(m), factor_steps(m)) if prep else (none, none, none)
                beside = [[none] * 4 + [c[0:2]],
                          [c[2:4], x, none, f, finish_steps(s, u) if fin else none]]
                for k in range(2):
                    for r in range(5):
                        quarter(s * GR + 2 * u + k, r, par, (2 * u + k) * HD, r < 4, r > 0, beside[k][r])

            dve.sem_inc(x1_ready, 1)
            dve.sem_inc(terms_made, C_TERMS)
            dve.sem_inc(out_ready, C_OUT)
            V.tensor_scalar(kinv_col[:], kinv_col[:], tg_x, None, ALU.mult).then_inc(prep_step, 10)
            prepare_rows(0)
            stages(dve, step, prepare, finish)

        @block.tensor
        def _(pe):
            T = nc.tensor

            def turn(s, par, u, groups):
                n = s * UP + u
                for g in groups:
                    if g % 2 == 0:
                        pe.wait_ge((cs_ready, q_ready)[g // 2], n + 2)
                    pe.wait_ge(turned_moved, C_MOVED + 4 * n + g - 1)
                    for a in range(4):
                        lt = (g % 2) * 4 + a
                        src = s_row[:, (NL - 1 - lt) * P:(NL - lt) * P] if g < 2 else s_row[:, lt * P:(lt + 1) * P]
                        ins = T.transpose(t_ps[g % 2][:, a, :], src, ident[:])
                    ins.then_inc(turned, 1)

            def prepare(s, par, u):
                turn(s, par, u, range(4))

            def finish(s, par, u):
                n = (s - 1) * UP + u
                pe.wait_ge(staged_ready, n + 1)
                pe.wait_ge(x1_ready, n + 1)
                for g in range(2):
                    for a in range(4):
                        ins = T.transpose(f_ps[g][:, a, :], staged[:, 4 * g + a, :], ident[:])
                    ins.then_inc(back, 1)

            def step(s, par, u, fin, prep, more):
                for k in range(2):
                    n = s * GR + 2 * u + k
                    pe.wait_ge(toep_in[k], 32 * (s * UP + u + 1))
                    pe.wait_ge(kvh_ready, 2 * n + 2)
                    pe.wait_ge(kvl_ready, C_LOW + 2 * n + 2)
                    for lt in range(NL):
                        pe.wait_ge(y_moved, C_YMOVED + NL * n + lt + 1 - YB)
                        for mt in range(lt + 1):
                            d = slice((lt - mt) * P, (lt - mt + 1) * P)
                            for q, (tp, kvp) in enumerate(((0, kvh), (0, kvl), (1, kvh))):
                                ins = T.matmul(y_ps[lt % YB][:, 0:COLS], toep[k][:, tp, d],
                                               kvp[k][:, mt].rearrange("p b r -> p (b r)"),
                                               start=(mt == 0 and q == 0), stop=(mt == lt and q == 2))
                        ins.then_inc(y_done, 1)
                        if lt == 3 and prep:
                            turn(s + 1, 1 - par, u, range(2 * k, 2 * k + 2))
                        if lt == 5 and k == 1 and fin:
                            finish(s, par, u)

            pe.sem_inc(turned, C_TURNED)
            pe.sem_inc(y_done, C_DONE)
            pe.sem_inc(back, C_BACK)
            stages(pe, step, prepare, finish)


def experts(nc, v):
    B, S, L, TT, KSEL, DFF, SLOTS = (v[k] for k in ("B", "S", "L", "TT", "KSEL", "DFF", "SLOTS"))
    x1, wall, outr, tg_f, ident = (v[k] for k in ("x1", "wall", "outr", "tg_f", "ident"))
    W_r, b_r, W1, b1, W2, b2 = (v[k] for k in ("W_r", "b_r", "W1", "b1", "W2", "b2"))
    ST = KSEL // P
    TOK = 2 * ST
    NT = TOK * P
    PASSES = SLOTS // TOK
    KT = L // P
    FT = 4
    GROUPS = DFF // (FT * P)
    DH = L // 512
    CH = TOK * DH
    TILES = PASSES * GROUPS * FT
    C_WOUT = 2
    assert TT == TOK and CH == KT == 2 * TT
    NA, NB = 12, 10
    with ExitStack() as c:
        def sb(n, s, d=F32): return c.enter_context(nc.sbuf_tensor(n, s, d))
        def sem(n): return c.enter_context(nc.semaphore(n))
        xTh, xTl = (sb(n, [P, KT, NT], F32R) for n in ("xTh", "xTl"))
        hh, hl = (sb(n, [P, FT, NT], F32R) for n in ("hh", "hl"))
        hf = [sb(f"hf{k}", [P, NT]) for k in range(2)]
        acc = sb("acc", [P, TOK, L])
        w1r = [sb(f"w1r{k}", [P, KT, P]) for k in range(2)]
        w1h = [sb(f"w1h{k}", [P, KT, P], F32R) for k in range(2)]
        w1l = [sb(f"w1l{k}", [P, KT, P], F32R) for k in range(2)]
        w2r = [sb(f"w2r{k}", [P, L]) for k in range(2)]
        w2h, w2l = (sb(n, [P, FT, L], F32R) for n in ("w2h", "w2l"))
        b1c = sb("b1c", [P, DFF // P])
        get_row, put_row = sb("get_row", [P, TOK], I32), sb("put_row", [P, TOK], I32)
        x1t = [sb(f"x1t{k}", [P, TT, L]) for k in range(2)]
        dl, xg = x1t
        slot_row = sb("slot_row", [P, SLOTS], I32)
        slot_gate, slot_mean, slot_rstd = (sb(n, [P, SLOTS]) for n in ("slot_gate", "slot_mean", "slot_rstd"))
        w_row = [sb(f"w_row{k}", [P, S]) for k in range(2)]
        w_col = [sb(f"w_col{k}", [P, TT]) for k in range(2)]
        wr_all = sb("wr_all", [P, L])
        br_all = sb("br_all", [P, 1])
        later = sb("later", [P, TT, S])
        slots_iota = sb("slots_iota", [P, KSEL])
        hot = sb("hot", [P, TT, KSEL])
        token = sb("token", [P, TT, 4])
        junk = sb("junk", [P, L])
        st = sb("rst", [P, TT, 2, 6])
        mv = [sb(f"mv{k}", [P, TT, 2]) for k in range(2)]
        rstd = [sb(f"rstd{k}", [P, TT]) for k in range(2)]
        var, std, dot, tmp = (sb(n, [P, TT]) for n in ("rvar", "std", "dot", "rtmp"))
        ge, eq, rank, sel, share = (sb(n, [P, TT]) for n in ("ge", "eq", "rank", "sel", "share"))
        base_scale, base_shift = sb("base_scale", [P, TT]), sb("base_shift", [P, TT])
        h_ps = [c.enter_context(nc.psum_tensor(f"h_ps{k}", [P, NT], F32)) for k in range(2)]
        t_ps = [c.enter_context(nc.psum_tensor(f"xt_ps{k}", [P, NT], F32)) for k in range(2)]
        o_ps = [c.enter_context(nc.psum_tensor(f"o_ps{k}", [P, 512], F32)) for k in range(TOK)]
        s_ps = t_ps[0][:, 0:4 * ST].rearrange("p (j c) -> p j c", c=4)

        bias_in = sem("bias_in")
        w1_in, w2_in = [sem(f"w1_in{k}") for k in range(2)], [sem(f"w2_in{k}") for k in range(2)]
        w1h_ready, w1l_ready, w2h_ready, w2l_ready = (sem(n) for n in ("w1h_ready", "w1l_ready", "w2h_ready", "w2l_ready"))
        h_done, gelu_done, hh_ready, hl_ready = (sem(n) for n in ("h_done", "gelu_done", "hh_ready", "hl_ready"))
        o_done, o_moved = sem("o_done"), sem("o_moved")
        rows_known, xg_in, xg_ready = sem("rows_known"), sem("xg_in"), sem("xg_ready")
        turned, xh_ready, xl_ready = sem("xturned"), sem("xh_ready"), sem("xl_ready")
        acc_ready, dl_ready, put, put_known = sem("acc_ready"), sem("dl_ready"), sem("put"), sem("put_known")
        passed = sem("xpassed")
        wr_in, x1_in, base_out = sem("wr_in"), [sem(f"x1_in{k}") for k in range(2)], sem("base_out")
        w_out, w_in = sem("w_out"), sem("w_in")
        const_step, const_ready = sem("const_step"), sem("const_ready")
        a_step, b_step = sem("a_step"), sem("b_step")
        var_ready, std_ready, w_ready = sem("rvar_ready"), sem("rstd_ready"), sem("w_ready")
        hot_ready, slots_done, slots_read = sem("hot_ready"), sem("slots_done"), sem("slots_read")
        share_ready, base_ready = sem("share_ready"), sem("base_ready")
        block = c.enter_context(nc.Block())
        w1_view = W1.rearrange("(k p) f -> p k f", p=P)

        def passes(engine, begin, group):
            begin()
            with engine.Fori(0, PASSES - 1) as p:
                for k in range(2):
                    group(p, k, False, True, weighs=k)
                for k in range(2):
                    group(p, 2 + k, False, True, places=k)
                with engine.Fori(4, GROUPS - 1) as g:
                    group(p, g, False, True)
                group(p, GROUPS - 1, True, True)
            with engine.Fori(0, GROUPS - 1) as g:
                group(PASSES - 1, g, False, False)
            group(PASSES - 1, GROUPS - 1, True, False)

        def tiles(t, b):
            return t[bass.ds(b * S, S), :].rearrange("(t p) l -> p t l", p=P)

        @block.sync
        def _(sp):
            def load(F, k):
                f = F % (GROUPS * FT)
                sp.wait_ge(w1l_ready, C_WOUT + F - 1)
                sp.dma_start(w1r[k][:], w1_view[:, :, bass.ds(f * P, P)]).then_inc(w1_in[k], 16)
                sp.wait_ge(w2l_ready, C_WOUT + F - 1)
                sp.dma_start(w2r[k][:], W2[bass.ds(f * P, P), :]).then_inc(w2_in[k], 16)

            def group(p, g, last, more, weighs=None, places=None):
                for f in range(FT):
                    load((p * GROUPS + g) * FT + f + 1, (f + 1) % 2)

            sp.dma_start(wr_all[:], bass.AP(W_r.tensor, 0, [[0, P], [1, L]])).then_inc(wr_in, 16)
            sp.dma_start(br_all[:], bass.AP(b_r.tensor, 0, [[0, P], [1, 1]])).then_inc(wr_in, 16)
            with nc.allow_non_contiguous_dma("b1 by hidden unit"):
                sp.dma_start(b1c[:], b1.rearrange("(c p) -> p c", p=P)).then_inc(bias_in, 16)
            passes(sp, lambda: load(0, 0), group)
            sp.wait_ge(w1_in[0], 16 * (TILES // 2 + 1))
            sp.wait_ge(w2_in[0], 16 * (TILES // 2 + 1))

        @block.gpsimd
        def _(pool):
            G = nc.gpsimd

            def constants():
                index = junk[:].bitcast(I32)
                G.memset(later[:], 1.0).then_inc(const_step, 1)
                G.iota(index[:, 0:KSEL], pattern=[[1, KSEL]], base=0, channel_multiplier=0).then_inc(const_step, 1)
                G.iota(index[:, KSEL:KSEL + TT], pattern=[[P, TT]], base=-S, channel_multiplier=1).then_inc(const_step, 1)
                pool.wait_ge(const_step, 3)
                G.affine_select(out=later[:], in_=later[:], compare_op=ALU.is_ge, fill=0.0, base=0,
                                pattern=[[-P, TT], [1, S]], channel_multiplier=-1).then_inc(const_ready, 1)
                G.tensor_copy(slots_iota[:], index[:, 0:KSEL]).then_inc(const_ready, 1)
                G.tensor_copy(token[:, :, 0], index[:, KSEL:KSEL + TT]).then_inc(const_ready, 1)

            def load_rows(b, k):
                settle(pool, passed)
                G.dma_start(x1t[k][:], tiles(x1, b)).then_inc(x1_in[k], 16)

            def spread_weights(b, k):
                pool.wait_ge(w_ready, b + 1)
                settle(pool, passed)
                with nc.allow_non_contiguous_dma("512 words"):
                    G.dma_start(wall[bass.ds(b, 1), :].rearrange("a (t p) -> p (a t)", p=P), w_col[k][:]).then_inc(w_out, 16)
                pool.wait_ge(w_out, 16 * b + 16)
                settle(pool, passed)
                G.dma_start(w_row[k][:], bass.AP(wall.tensor, b * S, [[0, P], [1, S]])).then_inc(w_in, 16)

            def store_base(b, k):
                pool.wait_ge(base_ready, b + 2)
                settle(pool, passed)
                G.dma_start(tiles(outr, b), x1t[k][:]).then_inc(base_out, 16)

            def route(p):
                for k in range(2):
                    spread_weights(2 * p + k, k)
                for k in range(2):
                    store_base(2 * p + k, k)
                pool.wait_ge(base_out, 32 * p + 32)

            def gather(p):
                pool.wait_ge(slots_read, 2 * p + 3)
                G.tensor_copy(get_row[:], slot_row[:, bass.ds(p * TOK, TOK)]).then_inc(rows_known, 1)
                pool.wait_ge(rows_known, p + 1)
                settle(pool, passed)
                for q in range(TOK):
                    G.indirect_dma_start(out=xg[:, q, :], out_offset=None, in_=x1,
                                         in_offset=bass.IndirectOffsetOnAxis(ap=get_row[:, q:q + 1], axis=0)
                                         ).then_inc(xg_in, 16)

            def start_sums():
                G.dma_start(acc[:], bass.AP(b2.tensor, 0, [[0, P], [0, TOK], [1, L]])).then_inc(acc_ready, 16)

            def scatter(p):
                for q in range(TOK):
                    G.indirect_dma_start(out=outr, out_offset=bass.IndirectOffsetOnAxis(ap=put_row[:, q:q + 1], axis=0),
                                         in_=dl[:, q, :], in_offset=None, compute_op=ALU.add).then_inc(put, 16)
                    pool.wait_ge(put, 16 * (TOK * p + q + 1))
                    settle(pool, passed)

            def a_pass(p, more):
                if more:
                    load_rows(2 * p + 2, 0)
                    pool.wait_ge(turned, KT * (p + 1) + 2)
                    load_rows(2 * p + 3, 1)
                    route(p + 1)
                    gather(p + 1)
                G.tensor_copy(put_row[:], slot_row[:, bass.ds(p * TOK, TOK)]).then_inc(put_known, 1)
                pool.wait_ge(put_known, p + 1)
                pool.wait_ge(dl_ready, TOK * (p + 1))
                settle(pool, passed)
                if more:
                    start_sums()
                scatter(p)

            pool.sem_inc(base_ready, 1)
            load_rows(0, 0)
            load_rows(1, 1)
            constants()
            route(0)
            gather(0)
            start_sums()
            with pool.Fori(0, PASSES - 1) as p:
                a_pass(p, True)
            a_pass(PASSES - 1, False)

        @block.scalar
        def _(act):
            A = nc.scalar

            def split_w1(F, k):
                act.wait_ge(w1_in[k], 16 * (F // 2) + 16)
                act.wait_ge(h_done, C_WOUT + F - 1)
                A.activation(w1h[k][:], w1r[k][:], ACT.Copy).then_inc(w1h_ready, 1)

            def turn_high(p, k):
                act.wait_ge(turned, KT * p + k + 1 + 2)
                A.activation(xTh[:, k, :], t_ps[k % 2][:], ACT.Copy).then_inc(xh_ready, 1)

            def deviations(b):
                act.wait_ge(var_ready, b + 1)
                A.activation(std[:], var[:], ACT.Sqrt).then_inc(std_ready, 1)

            def base(b, k):
                act.wait_ge(share_ready, b + 1)
                for t in range(TT):
                    ins = A.activation(x1t[k][:, t], x1t[k][:, t], ACT.Identity, bias=base_shift[:, t:t + 1],
                                       scale=base_scale[:, t:t + 1])
                ins.then_inc(base_ready, 1)

            def begin():
                split_w1(0, 0)
                for k in range(2):
                    deviations(k)
                for k in range(2):
                    base(k, k)
                for k in range(KT):
                    turn_high(0, k)

            def group(p, g, last, more, weighs=None, places=None):
                n = p * GROUPS + g
                for f in range(FT):
                    F = n * FT + f
                    split_w1(F + 1, (f + 1) % 2)
                    act.wait_ge(w2_in[f % 2], 16 * (F // 2) + 16)
                    if f == 0:
                        act.wait_ge(o_done, CH * n + TOK)
                    A.activation(w2h[:, f, :], w2r[f % 2][:], ACT.Copy).then_inc(w2h_ready, 1)
                    act.wait_ge(h_done, C_WOUT + F + 1)
                    act.wait_ge(hl_ready, C_WOUT + F - 1)
                    A.activation(hf[f % 2][:], h_ps[f % 2][:], ACT.Gelu_apprx_tanh,
                                 bias=b1c[:, bass.ds(g * FT + f, 1)]).then_inc(gelu_done, 1)
                    act.wait_ge(gelu_done, 2 + F + 1)
                    A.activation(hh[:, f, :], hf[f % 2][:], ACT.Copy).then_inc(hh_ready, 1)
                if weighs is not None:
                    deviations(2 * p + 2 + weighs)
                if places is not None:
                    base(2 * p + 2 + places, places)
                if last and more:
                    for k in range(KT):
                        turn_high(p + 1, k)

            act.wait_ge(bias_in, 16)
            passes(act, begin, group)

        @block.vector
        def _(dve):
            V = nc.vector
            ch = Chain(dve, a_step)
            cb = Chain(dve, b_step)

            def weigh(b, k, i):
                if i == 0:
                    ch.start(NA * b)
                    dve.wait_ge(x1_in[k], 16 * (b // 2) + 16)
                if i < TT:
                    V.bn_stats(st[:, i, 0, :], x1t[k][:, i, 0:512])
                    ins = V.bn_stats(st[:, i, 1, :], x1t[k][:, i, 512:1024])
                    if i == TT - 1:
                        ch.mark(ins)
                if i == TT:
                    ch.sync(); settle(dve, passed)
                    for t in range(TT):
                        ins = V.bn_aggr(mv[k][:, t, :], st[:, t].rearrange("p a b -> p (a b)"))
                    ch.mark(ins); ch.sync()
                    V.tensor_scalar(var[:], mv[k][:, :, 1], EPS, None, ALU.add).then_inc(var_ready, 1)
                if TT <= i < 2 * TT:
                    t = i - TT
                    ch.sync()
                    ch.mark(V.scalar_tensor_tensor(junk[:], x1t[k][:, t], mv[k][:, t, 0:1], wr_all[:],
                                                   ALU.subtract, ALU.mult, accum_out=dot[:, t:t + 1]))
                if i == 2 * TT:
                    ch.sync()
                    dve.wait_ge(std_ready, b + 1)
                    ch.mark(V.reciprocal(rstd[k][:], std[:])); ch.sync()
                    ch.mark(V.tensor_tensor(tmp[:], rstd[k][:], rstd[k][:], ALU.mult)); ch.sync()
                    ch.mark(V.tensor_tensor(tmp[:], tmp[:], var[:], ALU.mult)); ch.sync()
                    ch.mark(V.tensor_scalar(tmp[:], tmp[:], -0.5, 1.5, ALU.mult, ALU.add)); ch.sync()
                    ch.mark(V.tensor_tensor(rstd[k][:], rstd[k][:], tmp[:], ALU.mult)); ch.sync()
                    ch.mark(V.tensor_tensor(w_col[k][:], dot[:], rstd[k][:], ALU.mult)); ch.sync()
                    V.tensor_scalar(w_col[k][:], w_col[k][:], br_all[:, 0:1], None, ALU.add).then_inc(w_ready, 1)
                    dve.wait_ge(w_ready, b + 1)
                    assert ch.off == NA

            def place(b, k, i):
                if i == 0:
                    cb.start(NB * b)
                    dve.wait_ge(w_in, 16 * b + 16)
                if i < TT:
                    cb.sync()
                    V.tensor_scalar(junk[:, 0:S], w_row[k][:], w_col[k][:, i:i + 1], 0.0, ALU.is_ge, ALU.add,
                                    accum_out=ge[:, i:i + 1])
                    cb.mark(V.scalar_tensor_tensor(junk[:, S:2 * S], w_row[k][:], w_col[k][:, i:i + 1], later[:, i],
                                                   ALU.is_equal, ALU.mult, accum_out=eq[:, i:i + 1]))
                if i == TT:
                    dve.wait_ge(slots_done, b + 1)
                    V.tensor_scalar(token[:, :, 0], token[:, :, 0], float(S), None, ALU.add)
                    V.tensor_copy(token[:, :, 2], mv[k][:, :, 0])
                    V.tensor_copy(token[:, :, 3], rstd[k][:]); cb.sync()
                    V.tensor_tensor(rank[:], ge[:], eq[:], ALU.subtract)
                    cb.mark(V.tensor_scalar(sel[:], ge[:], KSEL - 0.5, None, ALU.is_le)); cb.sync()
                    for t in range(TT):
                        V.tensor_scalar(hot[:, t], slots_iota[:], rank[:, t:t + 1], None, ALU.is_equal)
                    V.tensor_tensor(token[:, :, 1], sel[:], w_col[k][:], ALU.mult).then_inc(hot_ready, 1)
                if i == TT + 1:
                    cb.mark(V.tensor_scalar(share[:], sel[:], -1.0, 1.0, ALU.mult, ALU.add)); cb.sync()
                    cb.mark(V.tensor_scalar(share[:], share[:], tg_f, None, ALU.mult)); cb.sync()
                    cb.mark(V.tensor_tensor(share[:], share[:], rstd[k][:], ALU.mult)); cb.sync()
                    dve.wait_ge(base_ready, b + 1)
                    cb.mark(V.tensor_scalar(base_scale[:], share[:], 1.0, None, ALU.add))
                    V.scalar_tensor_tensor(base_shift[:], share[:], -1.0, mv[k][:, :, 0], ALU.mult, ALU.mult).then_inc(share_ready, 1)
                if i == 2 * TT:
                    dve.wait_ge(share_ready, b + 1)
                    dve.wait_ge(slots_done, b + 2)
                    new = bass.ds(ST * b, ST)
                    V.tensor_copy(slot_row[:, new], s_ps[:, :, 0])
                    V.tensor_copy(slot_mean[:, new], s_ps[:, :, 2])
                    V.tensor_copy(slot_rstd[:, new], s_ps[:, :, 3])
                    cb.mark(V.tensor_scalar(slot_gate[:, new], s_ps[:, :, 1], tg_f, None, ALU.mult))
                    cb.sync()
                    dve.sem_inc(slots_read, 1)
                    assert cb.off == NB

            def split_w1(F, k):
                dve.wait_ge(w1h_ready, F + 1)
                V.tensor_tensor(w1l[k][:], w1r[k][:], w1h[k][:].bitcast(F32), ALU.subtract).then_inc(w1l_ready, 1)

            def normalize(p):
                dve.wait_ge(xg_in, 16 * TOK * (p + 1))
                for q in range(TOK):
                    one = bass.ds(p * TOK + q, 1)
                    ins = V.tensor_scalar(xg[:, q, :], xg[:, q, :], slot_mean[:, one], slot_rstd[:, one],
                                          ALU.subtract, ALU.mult)
                ins.then_inc(xg_ready, 1)

            def turn_low(p, k):
                dve.wait_ge(xh_ready, KT * p + k + 1)
                V.tensor_tensor(xTl[:, k, :], t_ps[k % 2][:], xTh[:, k, :].bitcast(F32), ALU.subtract).then_inc(xl_ready, 1)

            def begin():
                dve.wait_ge(const_ready, 3)
                dve.wait_ge(wr_in, 32)
                split_w1(0, 0)
                for k in range(2):
                    for i in range(CH + 1):
                        weigh(k, k, i)
                for k in range(2):
                    for i in range(CH + 1):
                        place(k, k, i)
                normalize(0)
                for k in range(KT):
                    turn_low(0, k)

            def group(p, g, last, more, weighs=None, places=None):
                n = p * GROUPS + g

                def beside(i):
                    if weighs is not None:
                        weigh(2 * p + 2 + weighs, weighs, i)
                    if places is not None:
                        place(2 * p + 2 + places, places, i)

                for f in range(FT):
                    F = n * FT + f
                    split_w1(F + 1, (f + 1) % 2)
                    dve.wait_ge(w2h_ready, F + 1)
                    V.tensor_tensor(w2l[:, f, :], w2r[f % 2][:], w2h[:, f, :].bitcast(F32), ALU.subtract).then_inc(w2l_ready, 1)
                    dve.wait_ge(hh_ready, F + 1)
                    V.tensor_tensor(hl[:, f, :], hf[f % 2][:], hh[:, f, :].bitcast(F32), ALU.subtract).then_inc(hl_ready, 1)
                dve.wait_ge(acc_ready, 16 * p + 16)
                turns = last and more
                for i in range(CH):
                    if turns and i == 0:
                        normalize(p + 1)
                        for k in range(TOK):
                            turn_low(p + 1, k)
                    a = acc[:, i % TOK, (i // TOK) * 512:(i // TOK + 1) * 512]
                    dve.wait_ge(o_done, TOK + CH * n + i + 1)
                    V.tensor_tensor(a, a, o_ps[i % TOK][:], ALU.add).then_inc(o_moved, 1)
                    beside(i)
                    if turns and i >= TOK:
                        turn_low(p + 1, i)
                dve.wait_ge(o_moved, TOK + CH * (n + 1))
                beside(CH)
                if last:
                    if not more:
                        dve.wait_ge(put, 16 * TOK * (PASSES - 1))
                    for q in range(TOK):
                        V.tensor_scalar(dl[:, q, :], acc[:, q, :], slot_gate[:, bass.ds(p * TOK + q, 1)], None,
                                        ALU.mult).then_inc(dl_ready, 1)

            dve.sem_inc(slots_read, 1)
            passes(dve, begin, group)

        @block.tensor
        def _(pe):
            T = nc.tensor

            def slots(b):
                pe.wait_ge(hot_ready, b + 1)
                pe.wait_ge(slots_read, b + 1)
                for j in range(ST):
                    for t in range(TT):
                        ins = T.matmul(s_ps[:, j, :], hot[:, t, j * P:(j + 1) * P], token[:, t, :],
                                       start=(t == 0), stop=(t == TT - 1))
                ins.then_inc(slots_done, 1)

            def turn(p, k):
                if k == 0:
                    pe.wait_ge(xg_ready, p + 1)
                pe.wait_ge(xl_ready, KT * p + k + 1)
                for q in range(TOK):
                    ins = T.transpose(t_ps[k % 2][:, q * P:(q + 1) * P], xg[:, q, k * P:(k + 1) * P], ident[:])
                ins.then_inc(turned, 1)

            def begin():
                slots(0)
                slots(1)
                for k in range(KT):
                    turn(0, k)

            def hidden(F, k):
                pe.wait_ge(w1l_ready, C_WOUT + F + 1)
                pe.wait_ge(gelu_done, 2 + F - 1)
                for kt in range(KT):
                    for j, (w, xx) in enumerate(((w1h, xTh), (w1h, xTl), (w1l, xTh))):
                        ins = T.matmul(h_ps[k][:], w[k][:, kt, :], xx[:, kt, :], start=(kt == 0 and j == 0),
                                       stop=(kt == KT - 1 and j == 2))
                ins.then_inc(h_done, 1)

            def down(i, fs, start, stop):
                q, d = i % TOK, i // TOK
                for f in fs:
                    for j, (ha, w) in enumerate(((hh, w2h), (hh, w2l), (hl, w2h))):
                        ins = T.matmul(o_ps[q][:], ha[:, f, q * P:(q + 1) * P], w[:, f, d * 512:(d + 1) * 512],
                                       start=(start and f == 0 and j == 0), stop=(stop and f == FT - 1 and j == 2))
                return ins

            def group(p, g, last, more, weighs=None, places=None):
                n = p * GROUPS + g
                pe.wait_ge(xl_ready, KT * (p + 1) + 2)
                for f in range(FT):
                    hidden(n * FT + f, f % 2)
                pe.wait_ge(hl_ready, C_WOUT + (n + 1) * FT - 1)
                pe.wait_ge(w2l_ready, C_WOUT + (n + 1) * FT - 1)
                for i in range(TOK):
                    pe.wait_ge(o_moved, CH * n + i + 1)
                    down(i, range(FT - 1), True, False)
                    if last and more:
                        turn(p + 1, i)
                pe.wait_ge(hl_ready, C_WOUT + (n + 1) * FT)
                pe.wait_ge(w2l_ready, C_WOUT + (n + 1) * FT)
                for i in range(TOK):
                    down(i, [FT - 1], False, True).then_inc(o_done, 1)
                for i in range(TOK, CH):
                    pe.wait_ge(o_moved, CH * n + i + 1)
                    down(i, range(FT), True, True).then_inc(o_done, 1)
                    if last and more:
                        turn(p + 1, i)
                if places is not None:
                    slots(2 * p + 2 + places)

            pe.sem_inc(xl_ready, 2)
            pe.sem_inc(turned, 2)
            pe.sem_inc(h_done, C_WOUT)
            pe.sem_inc(o_done, TOK)
            pe.sem_inc(o_moved, TOK)
            pe.sem_inc(gelu_done, 2)
            pe.sem_inc(hl_ready, C_WOUT)
            pe.sem_inc(w1l_ready, C_WOUT)
            pe.sem_inc(w2l_ready, C_WOUT)
            pe.sem_inc(slots_done, 1)
            passes(pe, begin, group)


_INS = ["x", "ctx_2048", "g_xattn", "g_ffn", "L0_xattn_ssm_kernel", "L0_xattn_D", "L0_ffn_W_r", "L0_ffn_b_r",
        "L0_ffn_W1", "L0_ffn_b1", "L0_ffn_W2", "L0_ffn_b2"]


def kernel(**inputs):
    import numpy as _np
    import concourse.bacc as _bacc
    from concourse import mybir as _mybir
    from concourse.bass_utils import run_bass_kernel_spmd as _run

    nc = _bacc.Bacc("TRN2", target_bir_lowering=False, num_devices=1)
    arrays, args = {}, []
    for name in _INS:
        a = _np.ascontiguousarray(inputs[name])
        arrays[f"in_{name}_dram"] = a
        args.append(nc.dram_tensor(f"in_{name}_dram", a.shape, _mybir.dt.from_np(a.dtype), kind="ExternalInput").ap())
    out = nc.dram_tensor("out_dram", inputs["x"].shape, _mybir.dt.float32, kind="ExternalOutput").ap()
    build(nc, *args, out)
    return _run(nc, [arrays], core_ids=[0]).results[0]["out_dram"]
```

```python
from contextlib import ExitStack

import concourse.bass as bass
from concourse import mybir

F32, F32R, F16, BF16, I32 = (mybir.dt.float32, mybir.dt.float32r, mybir.dt.float16, mybir.dt.bfloat16,
                              mybir.dt.int32)
ALU = mybir.AluOpType
ACT = mybir.ActivationFunctionType
AX_X = mybir.AxisListType.X
P = 128
EXPONENT = 0x7F800000
TINY = 1e-30
EPS = 1e-5


class Chain:

    def __init__(self, engine, sem):
        self.engine, self.sem, self.base, self.off = engine, sem, 0, 0

    def start(self, base):
        self.base, self.off = base, 0

    def mark(self, instruction):
        instruction.then_inc(self.sem, 1)
        self.off += 1
        return self.off

    def sync(self):
        self.engine.wait_ge(self.sem, self.base + self.off)


def settle(engine, passed):
    engine.sem_inc(passed, 1)


def build(nc, x, ctx, g_xattn, g_ffn, kern, D, W_r, b_r, W1, b1, W2, b2, out):
    B, S, L = x.shape
    H = kern.shape[0]
    HD = S // H
    GR = P // HD
    NG = H // GR
    BH = B // 2
    NL = L // P
    PAIRS = HD * (HD + 1) // 2
    COLS = BH * PAIRS
    LB = NL * BH
    HALF = NL // 2
    STAGES = 2 * NG
    PADK = P + L
    DFF = W1.shape[1]
    KSEL = 256
    TT = S // P
    SLOTS = B * KSEL // P

    kpad = nc.dram_tensor("kpad", [2, H, PADK], F16).ap()
    kinv = nc.dram_tensor("kinv", [H, HD], F32).ap()
    x1 = nc.dram_tensor("x1", [B * S, L], F32).ap()
    wall = nc.dram_tensor("wall", [B, S], F32).ap()
    xr = x.rearrange("b s l -> (b s) l")
    cr = ctx.rearrange("b s l -> (b s) l")
    outr = out.rearrange("b s l -> (b s) l")

    top = ExitStack()
    with top:
        ident = top.enter_context(nc.sbuf_tensor("ident", [P, P], F32))
        gates = top.enter_context(nc.sbuf_tensor("gates", [P, 4], F32))
        kinv_col = top.enter_context(nc.sbuf_tensor("kinv_col", [P, NG], F32))
        tg_x, tg_f = gates[:, 2:3], gates[:, 3:4]
        setup(nc, H, L, HD, PADK, NG, kern, D, g_xattn, g_ffn, kpad, kinv, ident, gates, kinv_col)
        conv(nc, locals())
        experts(nc, locals())


def setup(nc, H, L, HD, PADK, NG, kern, D, g_xattn, g_ffn, kpad, kinv, ident, gates, kinv_col):
    with ExitStack() as c:
        def sb(n, s, d): return c.enter_context(nc.sbuf_tensor(n, s, d))
        def sem(n): return c.enter_context(nc.semaphore(n))
        K = sb("K", [H, L], F32)
        Ks = sb("Ks", [H, L], F32)
        Dc = sb("Dc", [H, 1], F32)
        Kh = sb("Kh", [H, PADK], F16)
        Kl = sb("Kl", [H, PADK], F16)
        m = sb("km", [H, 4], F32)
        inv8 = sb("inv8", [H, HD], F32)
        inputs_in, gates_in = sem("inputs_in"), sem("gates_in")
        step, ident_ready = sem("setup_step"), sem("ident_ready")
        parts_ready, parts_out, inv_in = sem("parts_ready"), sem("parts_out"), sem("inv_in")
        tanh_done = sem("tanh_done")
        block = c.enter_context(nc.Block())

        @block.sync
        def _(sp):
            sp.dma_start(K[:], kern).then_inc(inputs_in, 16)
            sp.dma_start(Dc[:], D.rearrange("(h a) -> h a", a=1)).then_inc(inputs_in, 16)
            sp.dma_start(gates[:, 0:1], bass.AP(g_xattn.tensor, 0, [[0, P], [1, 1]])).then_inc(gates_in, 16)
            sp.dma_start(gates[:, 1:2], bass.AP(g_ffn.tensor, 0, [[0, P], [1, 1]])).then_inc(gates_in, 16)
            sp.wait_ge(parts_ready, 1)
            sp.dma_start(kpad[0], Kh[:]).then_inc(parts_out, 16)
            sp.dma_start(kpad[1], Kl[:]).then_inc(parts_out, 16)
            sp.dma_start(kinv, inv8[:]).then_inc(parts_out, 16)
            sp.wait_ge(parts_out, 48)
            with nc.allow_non_contiguous_dma("a few words"):
                sp.dma_start(kinv_col[:], bass.AP(kinv.tensor, 0, [[1, P], [P, NG]])).then_inc(inv_in, 16)
            sp.wait_ge(inv_in, 16)

        @block.scalar
        def _(act):
            act.wait_ge(gates_in, 32)
            nc.scalar.activation(gates[:, 2:4], gates[:, 0:2], ACT.Tanh).then_inc(tanh_done, 1)

        @block.gpsimd
        def _(pool):
            nc.gpsimd.memset(ident[:], 0.0).then_inc(ident_ready, 1)
            pool.wait_ge(ident_ready, 1)
            nc.gpsimd.affine_select(out=ident[:], in_=ident[:], compare_op=ALU.not_equal, fill=1.0, base=0,
                                    pattern=[[-1, P]], channel_multiplier=1).then_inc(ident_ready, 1)

        @block.vector
        def _(dve):
            ch = Chain(dve, step)
            V = nc.vector
            ch.mark(V.memset(Kh[:, 0:P], 0.0))
            ch.mark(V.memset(Kl[:, 0:P], 0.0))
            dve.wait_ge(inputs_in, 32)
            ch.mark(V.tensor_tensor(K[:, 0:1], K[:, 0:1], Dc[:], ALU.add)); ch.sync()
            ch.mark(V.tensor_reduce(m[:, 0:1], K[:], AX_X, ALU.max, apply_absolute_value=True)); ch.sync()
            ch.mark(V.tensor_scalar(m[:, 1:2], m[:, 0:1], TINY, None, ALU.max)); ch.sync()
            ch.mark(V.tensor_scalar(m[:, 2:3].bitcast(I32), m[:, 1:2].bitcast(I32), EXPONENT, None,
                                    ALU.bitwise_and)); ch.sync()
            ch.mark(V.reciprocal(m[:, 3:4], m[:, 2:3])); ch.sync()
            ch.mark(V.tensor_scalar(Ks[:], K[:], m[:, 3:4], 8192.0, ALU.mult, ALU.mult)); ch.sync()
            ch.mark(V.tensor_copy(Kh[:, P:PADK], Ks[:])); ch.sync()
            ch.mark(V.tensor_tensor(Kl[:, P:PADK], Ks[:], Kh[:, P:PADK], ALU.subtract))
            ch.mark(V.memset(inv8[:], 1.0 / 8192.0)); ch.sync()
            V.tensor_scalar(inv8[:], inv8[:], m[:, 2:3], None, ALU.mult).then_inc(parts_ready, 1)


def conv(nc, v):
    B, S, L, H, HD, GR, NG, BH, NL = (v[k] for k in ("B", "S", "L", "H", "HD", "GR", "NG", "BH", "NL"))
    PAIRS, COLS, HALF, STAGES, PADK = (v[k] for k in ("PAIRS", "COLS", "HALF", "STAGES", "PADK"))
    kpad, x1, xr, cr = (v[k] for k in ("kpad", "x1", "xr", "cr"))
    ident, kinv_col, tg_x = v["ident"], v["kinv_col"], v["tg_x"]
    HLB = HALF * BH
    QLB = HLB // 2
    FULL = HD // 2
    WRAP = HD + FULL - 1
    assert PAIRS == FULL * HD + FULL
    LB = NL * BH
    YB = 4
    UP = GR // 2
    assert UP == BH
    C_TURNED, C_MOVED, C_DONE, C_YMOVED, C_TERMS, C_LOW, C_BACK, C_KV, C_OUT = 4, 2, 2 * NL, YB, 4, 2, 2, 2, 2
    with ExitStack() as c:
        def sb(n, s, d): return c.enter_context(nc.sbuf_tensor(n, s, d))
        def pb(n, s): return c.enter_context(nc.psum_tensor(n, s, F32))
        def sem(n): return c.enter_context(nc.semaphore(n))
        ctxT_all = sb("ctxT", [P, 2, NL, BH, P], F32)
        ctxT = [ctxT_all[:, k] for k in range(2)]
        qT = [sb(f"qT{k}", [P, NL, BH, P], F32) for k in range(2)]
        kv = [sb(f"kv{k}", [P, HALF, BH, PAIRS], F32) for k in range(2)]
        kvh = [sb(f"kvh{k}", [P, NL, BH, PAIRS], F16) for k in range(2)]
        kvl = [sb(f"kvl{k}", [P, NL, BH, PAIRS], F16) for k in range(2)]
        y = [sb(f"y{k}", [P, HALF, BH, PAIRS], F32) for k in range(2)]
        cx = [sb(f"cx{k}", [P, HLB, WRAP], F32) for k in range(2)]
        qx = [sb(f"qx{k}", [P, HLB, WRAP], F32) for k in range(2)]
        prod = [sb(f"prod{k}", [P, QLB, HD * HD], F32) for k in range(2)]
        toep = [sb(f"toep{k}", [P, 2, L], F16) for k in range(2)]
        c_row = sb("c_row", [P, L], F32)
        x_row = sb("x_row", [P, L], F32)
        s_row = sb("s_row", [P, L], F32)
        f_row = sb("f_row", [P, L], F32)
        staged = sb("staged", [P, NL, P], F32)
        coef = sb("coef", [P, 3, BH], F32)
        st = sb("st", [P, 2, 6], F32)
        sc = sb("sc", [P, 12], F32)
        y_ps = [pb(f"y_ps{k}", [P, 512]) for k in range(YB)]
        t_ps = [pb(f"t_ps{k}", [P, 4, P]) for k in range(2)]
        f_ps = [pb(f"f_ps{k}", [P, 4, P]) for k in range(2)]

        ctx_in, x_in, fx_in, x1_out = sem("ctx_in"), sem("x_in"), sem("fx_in"), sem("x1_out")
        passed = sem("passed")
        toep_in = [sem(f"toep_in{k}") for k in range(2)]
        sum_step, prep_step = sem("sum_step"), sem("prep_step")
        var_ready, std_ready = sem("var_ready"), sem("std_ready")
        cs_ready, q_ready = sem("cs_ready"), sem("q_ready")
        cx_ready, cscale_ready, qscale_ready = sem("cx_ready"), sem("cscale_ready"), sem("qscale_ready")
        turned, turned_moved = sem("turned"), sem("turned_moved")
        kv_ready, kvh_ready, kvl_ready = sem("kv_ready"), sem("kvh_ready"), sem("kvl_ready")
        y_done, y_moved = sem("y_done"), sem("y_moved")
        terms_made = sem("terms_made")
        out_ready, staged_ready, back, x1_ready = sem("out_ready"), sem("staged_ready"), sem("back"), sem("x1_ready")
        block = c.enter_context(nc.Block())
        x_rows, f_rows = [x_row, f_row], [f_row, x_row]

        def stages(engine, step, prepare, finish, begin=None, begin_last=None):
            if prepare:
                with engine.Fori(0, UP // 2) as v:
                    for k in range(2):
                        prepare(0, 0, 2 * v + k, k)
            if begin:
                begin()
            with engine.Fori(0, UP) as u:
                step(0, 0, u, False, True, True)
            with engine.Fori(0, (STAGES - 2) // 2) as sp:
                for k in range(2):
                    with engine.Fori(0, UP) as u:
                        step(2 * sp + (1 + k), (k + 1) % 2, u, True, True, True)
            with engine.Fori(0, UP - 1) as u:
                step(STAGES - 1, (STAGES - 1) % 2, u, True, False, True)
            step(STAGES - 1, (STAGES - 1) % 2, UP - 1, True, False, False)
            if begin_last:
                begin_last()
            if finish:
                with engine.Fori(0, UP // 2) as v:
                    for k in range(2):
                        finish(STAGES, STAGES % 2, 2 * v + k, k)

        def slide(t, shape, first=0):
            whole = t[:]
            step = whole.ap[0][0]
            return bass.AP(whole.tensor, whole.offset + first * WRAP, [[step, P], [WRAP, shape[1]], [1, shape[2]], [1, shape[3]]])

        def rows(t, s, u):
            first = ((s // NG) * BH + u) * S + (s % NG) * P
            return t[bass.ds(first, P), :]

        @block.sync
        def _(sp):
            def load_ctx(m):
                sp.wait_ge(cs_ready, m + 1)
                sp.dma_start(c_row[:], rows(cr, (m // UP) % STAGES, m % UP)).then_inc(ctx_in, 16)

            def load_x(m, row):
                sp.dma_start(row[:], rows(xr, (m // UP) % STAGES, m % UP)).then_inc(x_in, 16)

            def kernels(n, k):
                h = ((n // GR) % NG) * GR + n % GR
                for part in range(2):
                    src = bass.AP(kpad.tensor, (h + part * H) * PADK + 1, [[1, P], [1, L]])
                    sp.dma_start(toep[k][:, part, :], src).then_inc(toep_in[k], 16)

            def fetch(s, par, u):
                n = (s - 1) * UP + u
                sp.wait_ge(x1_out, 16 * n + 16)
                sp.dma_start(f_row[:], rows(xr, s - 1, u)).then_inc(fx_in, 16)

            def store(s, par, u):
                n = (s - 1) * UP + u
                sp.wait_ge(x1_ready, 1 + n + 1)
                sp.dma_start(rows(x1, s - 1, u), f_row[:]).then_inc(x1_out, 16)

            def step(s, par, u, fin, prep, more):
                if fin:
                    fetch(s, par, u)
                for k in range(2):
                    n = s * GR + 2 * u + k
                    if more:
                        sp.wait_ge(y_done, C_DONE + NL * n + NL)
                        kernels(n + 2, k)
                    if k == 0 and prep:
                        m = (s + 1) * UP + u + 1
                        load_ctx(m)
                        sp.wait_ge(q_ready, m + 1)
                        load_x(m, x_row)
                if fin:
                    store(s, par, u)

            def begin():
                load_ctx(0)
                load_x(0, x_rows[0])
                sp.wait_ge(x_in, 16)
                load_x(1, x_rows[1])

                def ahead(u, k, more):
                    load_ctx(u + 1)
                    if more:
                        sp.wait_ge(q_ready, u + 2)
                        sp.wait_ge(x_in, 16 * u + 32)
                        load_x(u + 2, x_rows[k])

                with sp.Fori(0, UP // 2 - 1) as v:
                    for k in range(2):
                        ahead(2 * v + k, k, True)
                ahead(UP - 2, 0, True)
                ahead(UP - 1, 1, False)
                kernels(0, 0)
                kernels(1, 1)

            def last(s, par, u, k):
                n = (s - 1) * UP + u
                sp.wait_ge(x1_ready, 1 + n + 1)
                sp.dma_start(rows(x1, s - 1, u), f_rows[k][:]).then_inc(x1_out, 16)
                sp.wait_ge(x1_out, 16 * n + 32)
                sp.wait_ge(fx_in, 16 * n + 32)
                sp.dma_start(f_rows[k][:], rows(xr, s - 1, (u + 2) % UP)).then_inc(fx_in, 16)

            def fetch_first_two():
                n = (STAGES - 1) * UP
                sp.wait_ge(x1_out, 16 * n + 16)
                sp.dma_start(f_rows[0][:], rows(xr, STAGES - 1, 0)).then_inc(fx_in, 16)
                sp.wait_ge(var_ready, STAGES * UP + 1)
                sp.wait_ge(fx_in, 16 * n + 16)
                sp.dma_start(f_rows[1][:], rows(xr, STAGES - 1, 1)).then_inc(fx_in, 16)

            sp.sem_inc(x1_out, 16)
            stages(sp, step, None, last, begin, fetch_first_two)
            sp.wait_ge(fx_in, 16 * STAGES * UP + 32)
            sp.wait_ge(x1_out, 16 * STAGES * UP + 16)

        @block.gpsimd
        def _(pool):
            G = nc.gpsimd

            def step(s, par, u, fin, prep, more):
                for k in range(2):
                    n = s * GR + 2 * u + k

                    def products(half):
                        pool.wait_ge(cx_ready, 2 * n + half + 1)
                        pool.wait_ge(kvl_ready, C_LOW + 2 * n + half - 1)
                        dst = kv[half][:].rearrange("p a b r -> p (a b) r")
                        both = [P, HLB, FULL, HD]
                        G.tensor_tensor(dst[:, :, 0:FULL * HD].rearrange("p a (d i) -> p a d i", d=FULL),
                                        cx[half][:, :, 0:HD].rearrange("p a (d i) -> p a d i", d=1).broadcast_to(both),
                                        slide(cx[half], both), ALU.mult)
                        G.tensor_tensor(dst[:, :, FULL * HD:PAIRS], cx[half][:, :, 0:FULL], cx[half][:, :, FULL:HD],
                                        ALU.mult).then_inc(kv_ready, 1)

                    def low(half):
                        pool.wait_ge(kvh_ready, 2 * n + half + 1)
                        a = slice(half * HALF, (half + 1) * HALF)
                        G.tensor_tensor(kvl[k][:, a], kv[half][:], kvh[k][:, a], ALU.subtract).then_inc(kvl_ready, 1)

                    products(0)
                    products(1)
                    pool.wait_ge(y_done, C_DONE + NL * n - NL)
                    low(0)
                    low(1)

            pool.sem_inc(kvl_ready, C_LOW)
            pool.sem_inc(kv_ready, C_KV)
            stages(pool, step, None, None)

        @block.scalar
        def _(act):
            A = nc.scalar

            def root(m):
                act.wait_ge(var_ready, m + 1)
                A.activation(sc[:, 6:7], sc[:, 5:6], ACT.Sqrt).then_inc(std_ready, 1)

            def scale_ctx(m):
                act.wait_ge(cscale_ready, m + 1)
                act.wait_ge(turned, C_TURNED + 4 * m)
                A.activation(s_row[:, ::-1], c_row[:], ACT.Copy, scale=sc[:, 3:4]).then_inc(cs_ready, 1)

            def scale_x(m, row):
                act.wait_ge(qscale_ready, m + 1)
                act.wait_ge(turned, C_TURNED + 4 * m + 2)
                A.activation(s_row[:], row[:], ACT.Identity, bias=sc[:, 10:11], scale=sc[:, 9:10]).then_inc(q_ready, 1)

            def turn(s, par, u, groups):
                n = s * UP + u
                for g in groups:
                    dst = (ctxT if g < 2 else qT)[par]
                    a = (g % 2) * 4
                    act.wait_ge(turned, C_TURNED + 4 * n + g + 1)
                    settle(act, passed)
                    A.activation(dst[:, a:a + 4, bass.ds(u, 1), :].rearrange("p a b r -> p a (b r)"), t_ps[g % 2][:],
                                 ACT.Copy).then_inc(turned_moved, 1)

            def prepare(s, par, u, k):
                turn(s, par, u, range(2))
                scale_x(s * UP + u, x_rows[k])
                turn(s, par, u, range(2, 4))
                scale_ctx(s * UP + u + 1)
                root(s * UP + u + 1)

            def stage_out(s, par, u, k=0):
                n = (s - 1) * UP + u
                act.wait_ge(out_ready, C_OUT + 4 * GR * s)
                act.wait_ge(back, C_BACK + 2 * n)
                A.activation(staged[:], qT[1 - par][:, :, bass.ds(u, 1), :].rearrange("p a b r -> p a (b r)"),
                             ACT.Copy).then_inc(staged_ready, 1)

            def lay(dst, src, half, col):
                part = src[:, half * HALF:(half + 1) * HALF].rearrange("p a b r -> p (a b) r")
                A.activation(dst[half][:, :, 0:HD], part[:, :, bass.ds(col, HD)], ACT.Copy)
                return A.activation(dst[half][:, :, HD:WRAP], part[:, :, bass.ds(col, WRAP - HD)], ACT.Copy)

            def lay_ctx(n):
                first = ((n // GR) % 2) * (LB * P) + (n % GR) * HD
                for half in range(2):
                    act.wait_ge(kv_ready, C_KV + 2 * n + half - 1)
                    src = [bass.AP(ctxT_all[:].tensor, first + half * HLB * P, [[2 * LB * P, P], [P, HLB], [1, w]])
                           for w in (HD, WRAP - HD)]
                    A.activation(cx[half][:, :, 0:HD], src[0], ACT.Copy)
                    A.activation(cx[half][:, :, HD:WRAP], src[1], ACT.Copy).then_inc(cx_ready, 1)

            def high(n, k, half):
                if half == 0:
                    act.wait_ge(y_done, C_DONE + NL * n - NL)
                act.wait_ge(kv_ready, C_KV + 2 * n + half + 1)
                A.activation(kvh[k][:, half * HALF:(half + 1) * HALF], kv[half][:],
                             ACT.Copy).then_inc(kvh_ready, 1)

            def begin():
                act.wait_ge(turned_moved, C_MOVED + 4 * UP)
                lay_ctx(0)
                lay_ctx(1)
                high(0, 0, 0)
                high(0, 0, 1)

            def step(s, par, u, fin, prep, more):
                act.wait_ge(turned_moved, C_MOVED + 4 * UP * (s + 1))
                for k in range(2):
                    n = s * GR + 2 * u + k
                    for lt in range(NL):
                        half, a = lt // HALF, lt % HALF
                        if a == 0:
                            act.wait_ge(terms_made, C_TERMS + 4 * n + 2 * half - 2)
                            lay(qx, qT[par], half, (2 * u + k) * HD)
                        act.wait_ge(y_done, C_DONE + NL * n + lt + 1)
                        A.activation(y[half][:, a].rearrange("p b r -> p (b r)"), y_ps[lt % YB][:, 0:COLS],
                                     ACT.Copy).then_inc(y_moved, 1)
                        m = (s + 1) * UP + u
                        if lt == 3 and prep:
                            if k == 1 and fin:
                                act.wait_ge(staged_ready, (s - 1) * UP + u + 1)
                            turn(s + 1, 1 - par, u, range(2 * k, 2 * k + 2))
                        if lt in (3, 5) and (more or k == 0):
                            high(n + 1, 1 - k, lt // 4)
                        if lt == 5 and k == 0 and prep:
                            scale_x(m, x_row)
                        if lt == 6 and more:
                            if prep:
                                act.wait_ge(turned_moved, C_MOVED + 4 * UP * (s + 1) + 4 * u + 2)
                            lay_ctx(n + 2)
                    if k == 0 and fin:
                        stage_out(s, par, u)
                    if k == 1 and prep:
                        root(m + 1)
                        scale_ctx(m + 1)

            act.sem_inc(turned_moved, C_MOVED)
            act.sem_inc(y_moved, C_YMOVED)
            act.sem_inc(cs_ready, 1)
            act.sem_inc(q_ready, 1)
            scale_ctx(0)
            root(0)
            stages(act, step, prepare, stage_out, begin)

        @block.vector
        def _(dve):
            V = nc.vector

            def diagonal(t, first, rows, width):
                whole = t[:]
                return bass.AP(whole.tensor, whole.offset + first,
                               [[whole.ap[0][0], P], [HD * HD, QLB], [HD + 1, rows], [1, width]])

            def quarter(n, r, par, col, make, add, beside=()):
                Q = 4 * n + r
                half, t, b = r // 2, prod[r % 2], prod[(r - 1) % 2]
                a = slice((r % 2) * QLB, (r % 2 + 1) * QLB)
                both = [P, QLB, FULL, HD]
                small = iter(beside)

                def other():
                    for f in small:
                        f()
                        break

                if make:
                    q = qx[half][:, a]
                    ys = y[half][:].rearrange("p a b r -> p (a b) r")[:, a]
                    yd = ys[:, :, 0:FULL * HD].rearrange("p a (d i) -> p a d i", d=FULL)
                    if r % 2 == 0:
                        dve.wait_ge(y_moved, C_YMOVED + NL * n + HALF * (half + 1))
                    dve.wait_ge(out_ready, C_OUT + Q - 1)
                    V.tensor_tensor(t[:, :, 0:FULL * HD].rearrange("p a (d i) -> p a d i", d=FULL), yd,
                                    slide(qx[half], both, (r % 2) * QLB), ALU.mult)
                    other()
                if add:
                    dve.wait_ge(terms_made, C_TERMS + Q)
                    V.tensor_tensor(b[:, :, 0:32], b[:, :, 0:32], b[:, :, 32:64], ALU.add).then_inc(sum_step, 1)
                    other()
                if make:
                    V.tensor_tensor(diagonal(t, FULL * HD + 1, FULL - 1, HD), yd[:, :, 1:FULL],
                                    q[:, :, 0:HD].rearrange("p a (d i) -> p a d i", d=1)
                                    .broadcast_to([P, QLB, FULL - 1, HD]), ALU.mult)
                    other()
                if add:
                    dve.wait_ge(sum_step, 2 * Q - 1)
                    V.tensor_tensor(b[:, :, 0:16], b[:, :, 0:16], b[:, :, 16:32], ALU.add).then_inc(sum_step, 1)
                    other()
                if make:
                    V.tensor_tensor(t[:, :, HD * HD - FULL:HD * HD], ys[:, :, FULL * HD:PAIRS], q[:, :, 0:FULL], ALU.mult)
                    V.tensor_tensor(diagonal(t, FULL * HD, FULL, 1),
                                    ys[:, :, FULL * HD:PAIRS].rearrange("p a (d i) -> p a d i", i=1),
                                    q[:, :, FULL:HD].rearrange("p a (d i) -> p a d i", i=1), ALU.mult).then_inc(terms_made, 1)
                    other()
                if add:
                    dve.wait_ge(sum_step, 2 * Q)
                    lt = 2 * (r - 1)
                    o = qT[par][:, lt:lt + 2].rearrange("p a b r -> p (a b) r")
                    V.tensor_tensor(o[:, :, bass.ds(col, HD)], b[:, :, 0:HD], b[:, :, HD:2 * HD], ALU.add).then_inc(out_ready, 1)
                    other()

            ch = Chain(dve, prep_step)

            def ctx_in_steps(m):
                def largest():
                    ch.start(10 * m + 10)
                    ch.sync()
                    dve.wait_ge(ctx_in, 16 * m + 16)
                    dve.wait_ge(cs_ready, m + 1)
                    ch.mark(V.tensor_reduce(sc[:, 0:1], c_row[:], AX_X, ALU.max, apply_absolute_value=True))

                def above_zero():
                    ch.sync()
                    ch.mark(V.tensor_scalar(sc[:, 1:2], sc[:, 0:1], TINY, 1.0 / 64, ALU.max, ALU.mult))

                def power_of_two():
                    ch.sync()
                    ch.mark(V.tensor_scalar(sc[:, 2:3].bitcast(I32), sc[:, 1:2].bitcast(I32), EXPONENT, None,
                                            ALU.bitwise_and))

                def inverse():
                    ch.sync()
                    V.reciprocal(sc[:, 3:4], sc[:, 2:3]).then_inc(cscale_ready, 1)

                return largest, above_zero, power_of_two, inverse

            def x_in_steps(m, row=x_row):
                def first_half():
                    dve.wait_ge(x_in, 16 * m + 16)
                    V.bn_stats(st[:, 0, :], row[:, 0:512])

                def second_half():
                    ch.mark(V.bn_stats(st[:, 1, :], row[:, 512:1024]))

                def both_halves():
                    ch.sync(); settle(dve, passed)
                    ch.mark(V.bn_aggr(sc[:, 4:6], st[:].rearrange("p a b -> p (a b)")))

                def variance():
                    ch.sync()
                    V.tensor_scalar(sc[:, 5:6], sc[:, 5:6], EPS, None, ALU.add).then_inc(var_ready, 1)

                return first_half, second_half, both_halves, variance

            def factor_steps(m):
                def inverse():
                    dve.wait_ge(std_ready, m + 1)
                    dve.wait_ge(q_ready, m + 1)
                    ch.mark(V.reciprocal(sc[:, 6:7], sc[:, 6:7]))

                def square():
                    ch.sync()
                    ch.mark(V.tensor_scalar(sc[:, 7:8], sc[:, 6:7], sc[:, 6:7], sc[:, 5:6], ALU.mult, ALU.mult))

                def correction():
                    ch.sync()
                    ch.mark(V.tensor_scalar(sc[:, 8:9], sc[:, 7:8], -0.5, 1.5, ALU.mult, ALU.add))

                def factor():
                    ch.sync()
                    ch.mark(V.tensor_scalar(sc[:, 9:10], sc[:, 8:9], sc[:, 6:7], sc[:, 2:3], ALU.mult, ALU.mult))

                def shift():
                    ch.sync()
                    V.tensor_scalar(sc[:, 10:11], sc[:, 9:10], sc[:, 4:5], -1.0, ALU.mult, ALU.mult).then_inc(qscale_ready, 1)

                def scale_back():
                    ch.mark(V.tensor_scalar(coef[:, bass.ds((m // UP) % 3, 1), bass.ds(m % UP, 1)].rearrange("p a b -> p (a b)"),
                                            kinv_col[:, bass.ds((m // UP) % NG, 1)], sc[:, 2:3], None, ALU.mult))
                    assert ch.off == 10

                return inverse, square, correction, factor, shift, scale_back

            def prepare_rows(m, row):
                for f in ctx_in_steps(m) + x_in_steps(m, row) + factor_steps(m):
                    f()

            def prepare(s, par, u, k):
                prepare_rows(s * UP + u + 1, x_rows[1 - k])

            def finish_steps(s, u, row=f_row):
                n = (s - 1) * UP + u

                def bank(g):
                    a = slice(512 * g, 512 * (g + 1))
                    return V.scalar_tensor_tensor(row[:, a], f_ps[g][:].rearrange("p a b -> p (a b)"),
                                                  coef[:, bass.ds((s - 1) % 3, 1), bass.ds(u, 1)].rearrange("p a b -> p (a b)"),
                                                  row[:, a], ALU.mult, ALU.add)

                def first():
                    dve.wait_ge(x1_ready, 1 + n)
                    dve.wait_ge(fx_in, 16 * n + 16)
                    dve.wait_ge(back, C_BACK + 2 * n + 2)
                    bank(0)

                def second():
                    bank(1).then_inc(x1_ready, 1)

                return first, second

            def finish(s, par, u, k):
                for f in finish_steps(s, u, f_rows[k]):
                    f()

            def step(s, par, u, fin, prep, more):
                m = (s + 1) * UP + u + 1
                none = ()
                c, x, f = (ctx_in_steps(m), x_in_steps(m), factor_steps(m)) if prep else (none, none, none)
                beside = [[none] * 4 + [c[0:2]],
                          [c[2:4], x, none, f, finish_steps(s, u) if fin else none]]
                for k in range(2):
                    for r in range(5):
                        quarter(s * GR + 2 * u + k, r, par, (2 * u + k) * HD, r < 4, r > 0, beside[k][r])

            dve.sem_inc(x1_ready, 1)
            dve.sem_inc(terms_made, C_TERMS)
            dve.sem_inc(out_ready, C_OUT)
            V.tensor_scalar(kinv_col[:], kinv_col[:], tg_x, None, ALU.mult).then_inc(prep_step, 10)
            prepare_rows(0, x_row)
            stages(dve, step, prepare, finish)

        @block.tensor
        def _(pe):
            T = nc.tensor

            def turn(s, par, u, groups):
                n = s * UP + u
                for g in groups:
                    if g % 2 == 0:
                        pe.wait_ge((cs_ready, q_ready)[g // 2], n + 2)
                    pe.wait_ge(turned_moved, C_MOVED + 4 * n + g - 1)
                    for a in range(4):
                        lt = (g % 2) * 4 + a
                        src = s_row[:, (NL - 1 - lt) * P:(NL - lt) * P] if g < 2 else s_row[:, lt * P:(lt + 1) * P]
                        ins = T.transpose(t_ps[g % 2][:, a, :], src, ident[:])
                    ins.then_inc(turned, 1)

            def prepare(s, par, u, k):
                turn(s, par, u, range(4))

            def finish(s, par, u, k=0):
                n = (s - 1) * UP + u
                pe.wait_ge(staged_ready, n + 1)
                pe.wait_ge(x1_ready, n + 1)
                for g in range(2):
                    for a in range(4):
                        ins = T.transpose(f_ps[g][:, a, :], staged[:, 4 * g + a, :], ident[:])
                    ins.then_inc(back, 1)

            def step(s, par, u, fin, prep, more):
                for k in range(2):
                    n = s * GR + 2 * u + k
                    pe.wait_ge(toep_in[k], 32 * (s * UP + u + 1))
                    pe.wait_ge(kvh_ready, 2 * n + 2)
                    pe.wait_ge(kvl_ready, C_LOW + 2 * n + 2)
                    for lt in range(NL):
                        pe.wait_ge(y_moved, C_YMOVED + NL * n + lt + 1 - YB)
                        for mt in range(lt + 1):
                            d = slice((lt - mt) * P, (lt - mt + 1) * P)
                            for q, (tp, kvp) in enumerate(((0, kvh), (0, kvl), (1, kvh))):
                                ins = T.matmul(y_ps[lt % YB][:, 0:COLS], toep[k][:, tp, d],
                                               kvp[k][:, mt].rearrange("p b r -> p (b r)"),
                                               start=(mt == 0 and q == 0), stop=(mt == lt and q == 2))
                        ins.then_inc(y_done, 1)
                        if lt == 3 and prep:
                            turn(s + 1, 1 - par, u, range(2 * k, 2 * k + 2))
                        if lt == 5 and k == 1 and fin:
                            finish(s, par, u)

            pe.sem_inc(turned, C_TURNED)
            pe.sem_inc(y_done, C_DONE)
            pe.sem_inc(back, C_BACK)
            stages(pe, step, prepare, finish)


def experts(nc, v):
    B, S, L, TT, KSEL, DFF, SLOTS = (v[k] for k in ("B", "S", "L", "TT", "KSEL", "DFF", "SLOTS"))
    x1, wall, outr, tg_f, ident = (v[k] for k in ("x1", "wall", "outr", "tg_f", "ident"))
    W_r, b_r, W1, b1, W2, b2 = (v[k] for k in ("W_r", "b_r", "W1", "b1", "W2", "b2"))
    ST = KSEL // P
    TOK = 2 * ST
    NT = TOK * P
    PASSES = SLOTS // TOK
    KT = L // P
    FT = 4
    GROUPS = DFF // (FT * P)
    DH = L // 512
    CH = TOK * DH
    TILES = PASSES * GROUPS * FT
    RING = FT
    C_TWO, C_SPLIT = 2, RING
    assert TT == TOK and CH == KT == 2 * TT
    NA, NB = 12, 17
    with ExitStack() as c:
        def sb(n, s, d=F32): return c.enter_context(nc.sbuf_tensor(n, s, d))
        def sem(n): return c.enter_context(nc.semaphore(n))
        xTh, xTl = (sb(n, [P, KT, NT], F32R) for n in ("xTh", "xTl"))
        hh, hl = (sb(n, [P, FT, NT], F32R) for n in ("hh", "hl"))
        hf = [sb(f"hf{k}", [P, NT]) for k in range(2)]
        acc = sb("acc", [P, TOK, L])
        w1r = [sb(f"w1r{k}", [P, KT, P]) for k in range(RING)]
        w1h = [sb(f"w1h{k}", [P, KT, P], F32R) for k in range(2)]
        w1l = [sb(f"w1l{k}", [P, KT, P], F32R) for k in range(2)]
        w2r = [sb(f"w2r{k}", [P, L]) for k in range(RING)]
        w2h, w2l = (sb(n, [P, FT, L], F32R) for n in ("w2h", "w2l"))
        b1c = sb("b1c", [P, DFF // P])
        get_row, put_row = sb("get_row", [P, TOK], I32), sb("put_row", [P, TOK], I32)
        x1t = [sb(f"x1t{k}", [P, TT, L]) for k in range(2)]
        xg, dl = x1t
        slot_row = sb("slot_row", [P, SLOTS], I32)
        slot_gate, slot_mean, slot_rstd = (sb(n, [P, SLOTS]) for n in ("slot_gate", "slot_mean", "slot_rstd"))
        w_row = [sb(f"w_row{k}", [P, S]) for k in range(2)]
        w_col = [sb(f"w_col{k}", [P, TT]) for k in range(2)]
        wr_all = sb("wr_all", [P, L])
        br_all = sb("br_all", [P, 1])
        later = sb("later", [P, TT, S])
        slots_iota = sb("slots_iota", [P, KSEL])
        hot = sb("hot", [P, TT, KSEL], BF16)
        token = sb("token", [P, TT, 4])
        token_parts = sb("token_parts", [P, TT, 3, 4], BF16)
        rest = sb("rest", [P, TT, 4])
        found = sb("found", [P, ST, 4])
        junk = sb("junk", [P, L])
        st = sb("rst", [P, TT, 2, 6])
        mv = [sb(f"mv{k}", [P, TT, 2]) for k in range(2)]
        rstd = [sb(f"rstd{k}", [P, TT]) for k in range(2)]
        var, std, dot, tmp = (sb(n, [P, TT]) for n in ("rvar", "std", "dot", "rtmp"))
        ge, eq, rank, sel, share = (sb(n, [P, TT]) for n in ("ge", "eq", "rank", "sel", "share"))
        base_scale, base_shift = sb("base_scale", [P, TT]), sb("base_shift", [P, TT])
        h_ps = [c.enter_context(nc.psum_tensor(f"h_ps{k}", [P, NT], F32)) for k in range(2)]
        t_ps = [c.enter_context(nc.psum_tensor(f"xt_ps{k}", [P, NT], F32)) for k in range(2)]
        o_ps = [c.enter_context(nc.psum_tensor(f"o_ps{k}", [P, 512], F32)) for k in range(TOK)]
        s_ps = t_ps[0][:, 0:3 * 4 * ST].rearrange("p (j a c) -> p j a c", a=3, c=4)

        bias_in = sem("bias_in")
        w1_in, w2_in = [sem(f"w1_in{k}") for k in range(RING)], [sem(f"w2_in{k}") for k in range(RING)]
        w1h_ready, w1l_ready, w2h_ready, w2l_ready = (sem(n) for n in ("w1h_ready", "w1l_ready", "w2h_ready", "w2l_ready"))
        h_done, gelu_done, hh_ready, hl_ready = (sem(n) for n in ("h_done", "gelu_done", "hh_ready", "hl_ready"))
        o_done, o_moved = sem("o_done"), sem("o_moved")
        rows_known, xg_in, xg_ready = sem("rows_known"), sem("xg_in"), sem("xg_ready")
        turned, xh_ready, xl_ready = sem("xturned"), sem("xh_ready"), sem("xl_ready")
        acc_ready, dl_ready, put, put_known = sem("acc_ready"), sem("dl_ready"), sem("put"), sem("put_known")
        passed = sem("xpassed")
        wr_in, x1_in = sem("wr_in"), [sem(f"x1_in{k}") for k in range(2)]
        base_out, first_in = [sem(f"base_out{k}") for k in range(2)], [sem(f"first_in{k}") for k in range(2)]
        w_out, w_in = sem("w_out"), sem("w_in")
        const_step, const_ready = sem("const_step"), sem("const_ready")
        a_step, b_step = sem("a_step"), sem("b_step")
        var_ready, std_ready, w_ready = sem("rvar_ready"), sem("rstd_ready"), sem("w_ready")
        hot_ready, slots_done, slots_read = sem("hot_ready"), sem("slots_done"), sem("slots_read")
        share_ready, base_ready = sem("share_ready"), sem("base_ready")
        block = c.enter_context(nc.Block())
        w1_view = W1.rearrange("(k p) f -> p k f", p=P)

        def passes(engine, begin, group):
            begin()
            with engine.Fori(0, PASSES - 1) as p:
                group(p, 0, False, True)
                for k in range(2):
                    group(p, 1 + k, False, True, weighs=k)
                for k in range(2):
                    group(p, 3 + k, False, True, places=k)
                with engine.Fori(5, GROUPS - 1) as g:
                    group(p, g, False, True)
                group(p, GROUPS - 1, True, True)
            with engine.Fori(0, GROUPS - 1) as g:
                group(PASSES - 1, g, False, False)
            group(PASSES - 1, GROUPS - 1, True, False)

        def tiles(t, b):
            return t[bass.ds(b * S, S), :].rearrange("(t p) l -> p t l", p=P)

        @block.sync
        def _(sp):
            def load(F, k):
                f = F % (GROUPS * FT)
                sp.wait_ge(w1l_ready, C_SPLIT + F + 1 - RING)
                sp.dma_start(w1r[k][:], w1_view[:, :, bass.ds(f * P, P)]).then_inc(w1_in[k], 16)
                sp.wait_ge(w2l_ready, C_SPLIT + F + 1 - RING)
                sp.dma_start(w2r[k][:], W2[bass.ds(f * P, P), :]).then_inc(w2_in[k], 16)

            def group(p, g, last, more, weighs=None, places=None):
                for f in range(FT):
                    load((p * GROUPS + g) * FT + f + 1, (f + 1) % RING)

            def begin():
                for k in range(2):
                    sp.dma_start(x1t[k][:], tiles(x1, k)).then_inc(first_in[k], 16)
                sp.dma_start(wr_all[:], bass.AP(W_r.tensor, 0, [[0, P], [1, L]])).then_inc(wr_in, 16)
                sp.dma_start(br_all[:], bass.AP(b_r.tensor, 0, [[0, P], [1, 1]])).then_inc(wr_in, 16)
                load(0, 0)
                with nc.allow_non_contiguous_dma("b1 by hidden unit"):
                    sp.dma_start(b1c[:], b1.rearrange("(c p) -> p c", p=P)).then_inc(bias_in, 16)

            passes(sp, begin, group)
            sp.wait_ge(w1_in[0], 16 * (TILES // RING + 1))
            sp.wait_ge(w2_in[0], 16 * (TILES // RING + 1))

        @block.gpsimd
        def _(pool):
            G = nc.gpsimd

            def constants():
                index = junk[:].bitcast(I32)
                G.memset(later[:], 1.0).then_inc(const_step, 1)
                G.iota(index[:, 0:KSEL], pattern=[[1, KSEL]], base=0, channel_multiplier=0).then_inc(const_step, 1)
                G.iota(index[:, KSEL:KSEL + TT], pattern=[[P, TT]], base=-S, channel_multiplier=1).then_inc(const_step, 1)
                pool.wait_ge(const_step, 3)
                G.affine_select(out=later[:], in_=later[:], compare_op=ALU.is_ge, fill=0.0, base=0,
                                pattern=[[-P, TT], [1, S]], channel_multiplier=-1).then_inc(const_ready, 1)
                G.tensor_copy(slots_iota[:], index[:, 0:KSEL]).then_inc(const_ready, 1)
                G.tensor_copy(token[:, :, 0], index[:, KSEL:KSEL + TT]).then_inc(const_ready, 1)

            def load_rows(b, k):
                settle(pool, passed)
                G.dma_start(x1t[k][:], tiles(x1, b)).then_inc(x1_in[k], 16)

            def spread_weights(b, k):
                pool.wait_ge(w_ready, b + 1)
                settle(pool, passed)
                with nc.allow_non_contiguous_dma("512 words"):
                    G.dma_start(wall[bass.ds(b, 1), :].rearrange("a (t p) -> p (a t)", p=P), w_col[k][:]).then_inc(w_out, 16)
                pool.wait_ge(w_out, 16 * b + 16)
                settle(pool, passed)
                G.dma_start(w_row[k][:], bass.AP(wall.tensor, b * S, [[0, P], [1, S]])).then_inc(w_in, 16)

            def store_base(b, k):
                pool.wait_ge(base_ready, b + 2)
                settle(pool, passed)
                G.dma_start(tiles(outr, b), x1t[k][:]).then_inc(base_out[k], 16)

            def route(p):
                for k in range(2):
                    spread_weights(2 * p + k, k)
                for k in range(2):
                    store_base(2 * p + k, k)

            def gather(p):
                pool.wait_ge(slots_read, 2 * p + 3)
                pool.wait_ge(base_out[0], 16 * p + 16)
                G.tensor_copy(get_row[:], slot_row[:, bass.ds(p * TOK, TOK)]).then_inc(rows_known, 1)
                pool.wait_ge(rows_known, p + 1)
                settle(pool, passed)
                for q in range(TOK):
                    G.indirect_dma_start(out=xg[:, q, :], out_offset=None, in_=x1,
                                         in_offset=bass.IndirectOffsetOnAxis(ap=get_row[:, q:q + 1], axis=0)
                                         ).then_inc(xg_in, 16)

            def start_sums():
                G.dma_start(acc[:], bass.AP(b2.tensor, 0, [[0, P], [0, TOK], [1, L]])).then_inc(acc_ready, 16)

            def scatter(p):
                for q in range(TOK):
                    G.indirect_dma_start(out=outr, out_offset=bass.IndirectOffsetOnAxis(ap=put_row[:, q:q + 1], axis=0),
                                         in_=dl[:, q, :], in_offset=None, compute_op=ALU.add).then_inc(put, 16)
                    pool.wait_ge(put, 16 * (TOK * p + q + 1))
                    settle(pool, passed)

            def a_pass(p, more):
                if more:
                    pool.wait_ge(turned, KT * (p + 1) + 2)
                    load_rows(2 * p + 2, 0)
                    load_rows(2 * p + 3, 1)
                    route(p + 1)
                    gather(p + 1)
                G.tensor_copy(put_row[:], slot_row[:, bass.ds(p * TOK, TOK)]).then_inc(put_known, 1)
                pool.wait_ge(put_known, p + 1)
                pool.wait_ge(dl_ready, TOK * (p + 1))
                settle(pool, passed)
                if more:
                    start_sums()
                scatter(p)

            pool.sem_inc(base_ready, 1)
            constants()
            route(0)
            gather(0)
            start_sums()
            with pool.Fori(0, PASSES - 1) as p:
                a_pass(p, True)
            a_pass(PASSES - 1, False)

        @block.scalar
        def _(act):
            A = nc.scalar

            def split_w1(F, f):
                act.wait_ge(w1_in[f], 16 * (F // RING) + 16)
                act.wait_ge(h_done, C_TWO + F - 1)
                A.activation(w1h[f % 2][:], w1r[f][:], ACT.Copy).then_inc(w1h_ready, 1)

            def turn_high(p, k):
                act.wait_ge(turned, KT * p + k + 1 + 2)
                A.activation(xTh[:, k, :], t_ps[k % 2][:], ACT.Copy).then_inc(xh_ready, 1)

            def deviations(b):
                act.wait_ge(var_ready, b + 1)
                A.activation(std[:], var[:], ACT.Sqrt).then_inc(std_ready, 1)

            def base(b, k):
                act.wait_ge(share_ready, b + 1)
                for t in range(TT):
                    ins = A.activation(x1t[k][:, t], x1t[k][:, t], ACT.Identity, bias=base_shift[:, t:t + 1],
                                       scale=base_scale[:, t:t + 1])
                ins.then_inc(base_ready, 1)

            def begin():
                for k in range(2):
                    deviations(k)
                split_w1(0, 0)
                split_w1(1, 1)
                for k in range(2):
                    base(k, k)
                act.wait_ge(bias_in, 16)
                for k in range(KT):
                    turn_high(0, k)

            def group(p, g, last, more, weighs=None, places=None):
                n = p * GROUPS + g
                for f in range(FT):
                    F = n * FT + f
                    if f:
                        split_w1(F + 1, (f + 1) % FT)
                    act.wait_ge(w2_in[f], 16 * (F // RING) + 16)
                    if f == 0:
                        act.wait_ge(o_done, CH * n + TOK)
                    A.activation(w2h[:, f, :], w2r[f][:], ACT.Copy).then_inc(w2h_ready, 1)
                    act.wait_ge(h_done, C_TWO + F + 1)
                    act.wait_ge(hl_ready, C_TWO + F - 1)
                    A.activation(hf[f % 2][:], h_ps[f % 2][:], ACT.Gelu_apprx_tanh,
                                 bias=b1c[:, bass.ds(g * FT + f, 1)]).then_inc(gelu_done, 1)
                    act.wait_ge(gelu_done, 2 + F + 1)
                    A.activation(hh[:, f, :], hf[f % 2][:], ACT.Copy).then_inc(hh_ready, 1)
                if more or not last:
                    split_w1((n + 1) * FT + 1, 1)
                if weighs is not None:
                    deviations(2 * p + 2 + weighs)
                if places is not None:
                    base(2 * p + 2 + places, places)
                if last and more:
                    for k in range(KT):
                        turn_high(p + 1, k)

            passes(act, begin, group)

        @block.vector
        def _(dve):
            V = nc.vector
            ch = Chain(dve, a_step)
            cb = Chain(dve, b_step)

            def weigh(b, k, i, first=False):
                if i == 0:
                    ch.start(NA * b)
                    if first:
                        dve.wait_ge(first_in[k], 16)
                    else:
                        dve.wait_ge(x1_in[k], 16 * (b // 2))
                if i < TT:
                    V.bn_stats(st[:, i, 0, :], x1t[k][:, i, 0:512])
                    ins = V.bn_stats(st[:, i, 1, :], x1t[k][:, i, 512:1024])
                    if i == TT - 1:
                        ch.mark(ins)
                if i == TT:
                    ch.sync(); settle(dve, passed)
                    for t in range(TT):
                        ins = V.bn_aggr(mv[k][:, t, :], st[:, t].rearrange("p a b -> p (a b)"))
                    ch.mark(ins); ch.sync()
                    V.tensor_scalar(var[:], mv[k][:, :, 1], EPS, None, ALU.add).then_inc(var_ready, 1)
                if TT <= i < 2 * TT:
                    t = i - TT
                    ch.sync()
                    ch.mark(V.scalar_tensor_tensor(junk[:], x1t[k][:, t], mv[k][:, t, 0:1], wr_all[:],
                                                   ALU.subtract, ALU.mult, accum_out=dot[:, t:t + 1]))
                if i == 2 * TT:
                    ch.sync()
                    dve.wait_ge(std_ready, b + 1)
                    ch.mark(V.reciprocal(rstd[k][:], std[:])); ch.sync()
                    ch.mark(V.tensor_tensor(tmp[:], rstd[k][:], rstd[k][:], ALU.mult)); ch.sync()
                    ch.mark(V.tensor_tensor(tmp[:], tmp[:], var[:], ALU.mult)); ch.sync()
                    ch.mark(V.tensor_scalar(tmp[:], tmp[:], -0.5, 1.5, ALU.mult, ALU.add)); ch.sync()
                    ch.mark(V.tensor_tensor(rstd[k][:], rstd[k][:], tmp[:], ALU.mult)); ch.sync()
                    ch.mark(V.tensor_tensor(w_col[k][:], dot[:], rstd[k][:], ALU.mult)); ch.sync()
                    V.tensor_scalar(w_col[k][:], w_col[k][:], br_all[:, 0:1], None, ALU.add).then_inc(w_ready, 1)
                    dve.wait_ge(w_ready, b + 1)
                    assert ch.off == NA

            def place(b, k, i):
                if i == 0:
                    cb.start(NB * b)
                    dve.wait_ge(w_in, 16 * b + 16)
                if i < TT:
                    cb.sync()
                    V.tensor_scalar(junk[:, 0:S], w_row[k][:], w_col[k][:, i:i + 1], 0.0, ALU.is_ge, ALU.add,
                                    accum_out=ge[:, i:i + 1])
                    cb.mark(V.scalar_tensor_tensor(junk[:, S:2 * S], w_row[k][:], w_col[k][:, i:i + 1], later[:, i],
                                                   ALU.is_equal, ALU.mult, accum_out=eq[:, i:i + 1]))
                if i == TT:
                    dve.wait_ge(slots_done, b + 1)
                    V.tensor_scalar(token[:, :, 0], token[:, :, 0], float(S), None, ALU.add)
                    V.tensor_copy(token[:, :, 2], mv[k][:, :, 0])
                    V.tensor_copy(token[:, :, 3], rstd[k][:]); cb.sync()
                    V.tensor_tensor(rank[:], ge[:], eq[:], ALU.subtract)
                    cb.mark(V.tensor_scalar(sel[:], ge[:], KSEL - 0.5, None, ALU.is_le)); cb.sync()
                    for t in range(TT):
                        V.tensor_scalar(hot[:, t], slots_iota[:], rank[:, t:t + 1], None, ALU.is_equal)
                    cb.mark(V.tensor_tensor(token[:, :, 1], sel[:], w_col[k][:], ALU.mult)); cb.sync()
                    cb.mark(V.tensor_copy(token_parts[:, :, 0], token[:])); cb.sync()
                    cb.mark(V.tensor_tensor(rest[:], token[:], token_parts[:, :, 0], ALU.subtract)); cb.sync()
                    cb.mark(V.tensor_copy(token_parts[:, :, 1], rest[:])); cb.sync()
                    V.tensor_tensor(token_parts[:, :, 2], rest[:], token_parts[:, :, 1], ALU.subtract).then_inc(hot_ready, 1)
                if i == TT + 1:
                    cb.mark(V.tensor_scalar(share[:], sel[:], -1.0, 1.0, ALU.mult, ALU.add)); cb.sync()
                    cb.mark(V.tensor_scalar(share[:], share[:], tg_f, None, ALU.mult)); cb.sync()
                    cb.mark(V.tensor_tensor(share[:], share[:], rstd[k][:], ALU.mult)); cb.sync()
                    dve.wait_ge(base_ready, b + 1)
                    cb.mark(V.tensor_scalar(base_scale[:], share[:], 1.0, None, ALU.add))
                    V.scalar_tensor_tensor(base_shift[:], share[:], -1.0, mv[k][:, :, 0], ALU.mult, ALU.mult).then_inc(share_ready, 1)
                if i == 2 * TT:
                    dve.wait_ge(share_ready, b + 1)
                    dve.wait_ge(slots_done, b + 2)
                    new = bass.ds(ST * b, ST)
                    cb.mark(V.tensor_copy(found[:], s_ps[:, :, 2])); cb.sync()
                    cb.mark(V.tensor_tensor(found[:], found[:], s_ps[:, :, 1], ALU.add)); cb.sync()
                    cb.mark(V.tensor_tensor(found[:], found[:], s_ps[:, :, 0], ALU.add)); cb.sync()
                    V.tensor_copy(slot_row[:, new], found[:, :, 0])
                    V.tensor_copy(slot_mean[:, new], found[:, :, 2])
                    V.tensor_copy(slot_rstd[:, new], found[:, :, 3])
                    cb.mark(V.tensor_scalar(slot_gate[:, new], found[:, :, 1], tg_f, None, ALU.mult))
                    cb.sync()
                    dve.sem_inc(slots_read, 1)
                    assert cb.off == NB

            def split_w1(F, f):
                dve.wait_ge(w1h_ready, F + 1)
                V.tensor_tensor(w1l[f % 2][:], w1r[f][:], w1h[f % 2][:].bitcast(F32), ALU.subtract).then_inc(w1l_ready, 1)

            def normalize(p, q):
                one = bass.ds(p * TOK + q, 1)
                V.tensor_scalar(xg[:, q, :], xg[:, q, :], slot_mean[:, one], slot_rstd[:, one],
                                ALU.subtract, ALU.mult).then_inc(xg_ready, 1)

            def turn_low(p, k):
                dve.wait_ge(xh_ready, KT * p + k + 1)
                V.tensor_tensor(xTl[:, k, :], t_ps[k % 2][:], xTh[:, k, :].bitcast(F32), ALU.subtract).then_inc(xl_ready, 1)

            def begin():
                dve.wait_ge(const_ready, 3)
                dve.wait_ge(wr_in, 32)
                for k in range(2):
                    for i in range(CH + 1):
                        weigh(k, k, i, True)
                split_w1(0, 0)
                split_w1(1, 1)
                for k in range(2):
                    for i in range(CH + 1):
                        place(k, k, i)
                dve.wait_ge(xg_in, 16 * TOK)
                for q in range(TOK):
                    normalize(0, q)
                for k in range(KT):
                    turn_low(0, k)

            def group(p, g, last, more, weighs=None, places=None):
                n = p * GROUPS + g

                def beside(i):
                    if weighs is not None:
                        weigh(2 * p + 2 + weighs, weighs, i)
                    if places is not None:
                        place(2 * p + 2 + places, places, i)

                turns = last and more
                if turns:
                    dve.wait_ge(xg_in, 16 * TOK * (p + 2))
                for f in range(FT):
                    F = n * FT + f
                    if f:
                        split_w1(F + 1, (f + 1) % FT)
                    dve.wait_ge(w2h_ready, F + 1)
                    V.tensor_tensor(w2l[:, f, :], w2r[f][:], w2h[:, f, :].bitcast(F32), ALU.subtract).then_inc(w2l_ready, 1)
                    dve.wait_ge(hh_ready, F + 1)
                    V.tensor_tensor(hl[:, f, :], hf[f % 2][:], hh[:, f, :].bitcast(F32), ALU.subtract).then_inc(hl_ready, 1)
                    if turns:
                        normalize(p + 1, f)
                dve.wait_ge(acc_ready, 16 * p + 16)
                dve.wait_ge(o_moved, TOK + CH * n)
                if turns:
                    for k in range(TOK):
                        turn_low(p + 1, k)
                for i in range(CH):
                    if i == 0:
                        for part in range(3):
                            beside(part)
                    a = acc[:, i % TOK, (i // TOK) * 512:(i // TOK + 1) * 512]
                    dve.wait_ge(o_done, TOK + CH * n + i + 1)
                    V.tensor_tensor(a, a, o_ps[i % TOK][:], ALU.add).then_inc(o_moved, 1)
                    if i == 1 or i >= 3:
                        beside(3 if i == 1 else i + 1)
                    if turns and i in (TOK, TOK + 1):
                        turn_low(p + 1, 2 * i - TOK)
                        turn_low(p + 1, 2 * i - TOK + 1)
                    if i == CH - 2 and (more or not last):
                        split_w1((n + 1) * FT + 1, 1)
                if last:
                    dve.wait_ge(o_moved, TOK + CH * (n + 1))
                    if more:
                        dve.wait_ge(base_out[1], 16 * p + 32)
                    else:
                        dve.wait_ge(put, 16 * TOK * (PASSES - 1))
                    for q in range(TOK):
                        V.tensor_scalar(dl[:, q, :], acc[:, q, :], slot_gate[:, bass.ds(p * TOK + q, 1)], None,
                                        ALU.mult).then_inc(dl_ready, 1)

            dve.sem_inc(slots_read, 1)
            passes(dve, begin, group)

        @block.tensor
        def _(pe):
            T = nc.tensor

            def slots(b):
                pe.wait_ge(hot_ready, b + 1)
                pe.wait_ge(slots_read, b + 1)
                for j in range(ST):
                    for t in range(TT):
                        ins = T.matmul(s_ps[:, j].rearrange("p a c -> p (a c)"), hot[:, t, j * P:(j + 1) * P],
                                       token_parts[:, t].rearrange("p a c -> p (a c)"),
                                       start=(t == 0), stop=(t == TT - 1))
                ins.then_inc(slots_done, 1)

            def turn(p, k):
                if k == 0:
                    pe.wait_ge(xg_ready, TOK * (p + 1))
                pe.wait_ge(xl_ready, KT * p + k + 1)
                for q in range(TOK):
                    ins = T.transpose(t_ps[k % 2][:, q * P:(q + 1) * P], xg[:, q, k * P:(k + 1) * P], ident[:])
                ins.then_inc(turned, 1)

            def begin():
                slots(0)
                slots(1)
                for k in range(KT):
                    turn(0, k)

            def hidden(F, k):
                pe.wait_ge(w1l_ready, C_SPLIT + F + 1)
                pe.wait_ge(gelu_done, 2 + F - 1)
                for kt in range(KT):
                    for j, (w, xx) in enumerate(((w1h, xTh), (w1h, xTl), (w1l, xTh))):
                        ins = T.matmul(h_ps[k][:], w[k][:, kt, :], xx[:, kt, :], start=(kt == 0 and j == 0),
                                       stop=(kt == KT - 1 and j == 2))
                ins.then_inc(h_done, 1)

            def down(i, fs, start, stop):
                q, d = i % TOK, i // TOK
                for f in fs:
                    for j, (ha, w) in enumerate(((hh, w2h), (hh, w2l), (hl, w2h))):
                        ins = T.matmul(o_ps[q][:], ha[:, f, q * P:(q + 1) * P], w[:, f, d * 512:(d + 1) * 512],
                                       start=(start and f == 0 and j == 0), stop=(stop and f == FT - 1 and j == 2))
                return ins

            def group(p, g, last, more, weighs=None, places=None):
                n = p * GROUPS + g
                pe.wait_ge(xl_ready, KT * (p + 1) + 2)
                for f in range(FT):
                    hidden(n * FT + f, f % 2)
                pe.wait_ge(hl_ready, C_TWO + (n + 1) * FT - 1)
                pe.wait_ge(w2l_ready, C_SPLIT + (n + 1) * FT - 1)
                for i in range(TOK):
                    pe.wait_ge(o_moved, CH * n + i + 1)
                    down(i, range(FT - 1), True, False)
                    if last and more:
                        turn(p + 1, i)
                pe.wait_ge(hl_ready, C_TWO + (n + 1) * FT)
                pe.wait_ge(w2l_ready, C_SPLIT + (n + 1) * FT)
                for i in range(TOK):
                    down(i, [FT - 1], False, True).then_inc(o_done, 1)
                for i in range(TOK, CH):
                    pe.wait_ge(o_moved, CH * n + i + 1)
                    down(i, range(FT), True, True).then_inc(o_done, 1)
                    if last and more and i in (TOK, TOK + 1):
                        turn(p + 1, 2 * i - TOK)
                        turn(p + 1, 2 * i - TOK + 1)
                if places is not None:
                    slots(2 * p + 2 + places)

            pe.sem_inc(xl_ready, 2)
            pe.sem_inc(turned, 2)
            pe.sem_inc(h_done, C_TWO)
            pe.sem_inc(o_done, TOK)
            pe.sem_inc(o_moved, TOK)
            pe.sem_inc(gelu_done, 2)
            pe.sem_inc(hl_ready, C_TWO)
            pe.sem_inc(w1l_ready, C_SPLIT)
            pe.sem_inc(w2l_ready, C_SPLIT)
            pe.sem_inc(slots_done, 1)
            passes(pe, begin, group)


_INS = ["x", "ctx_2048", "g_xattn", "g_ffn", "L0_xattn_ssm_kernel", "L0_xattn_D", "L0_ffn_W_r", "L0_ffn_b_r",
        "L0_ffn_W1", "L0_ffn_b1", "L0_ffn_W2", "L0_ffn_b2"]


def kernel(**inputs):
    import numpy as _np
    import concourse.bacc as _bacc
    from concourse import mybir as _mybir
    from concourse.bass_utils import run_bass_kernel_spmd as _run

    nc = _bacc.Bacc("TRN2", target_bir_lowering=False, num_devices=1)
    arrays, args = {}, []
    for name in _INS:
        a = _np.ascontiguousarray(inputs[name])
        arrays[f"in_{name}_dram"] = a
        args.append(nc.dram_tensor(f"in_{name}_dram", a.shape, _mybir.dt.from_np(a.dtype), kind="ExternalInput").ap())
    out = nc.dram_tensor("out_dram", inputs["x"].shape, _mybir.dt.float32, kind="ExternalOutput").ap()
    build(nc, *args, out)
    return _run(nc, [arrays], core_ids=[0]).results[0]["out_dram"]
```
